# Optimizing a Trainium2 kernel written in Bass

```python
import numpy as np
import jax
import jax.numpy as jnp

def _softmax(x, axis=-1):
    return jax.nn.softmax(x, axis=axis)

def _gelu(x):
    return jax.nn.gelu(x, approximate=True)

def _silu(x):
    return jax.nn.silu(x)

def _sigmoid(x):
    return jax.nn.sigmoid(x)

def _layernorm(x, axis=-1, eps=1e-05):
    m = jnp.mean(x, axis=axis, keepdims=True)
    v = jnp.var(x, axis=axis, keepdims=True)
    return (x - m) / jnp.sqrt(v + eps)

def _scatter_add(tgt, idx, src, axis=0):
    return tgt.at[idx].add(src)

def _segment_sum(src, seg, n):
    return jax.ops.segment_sum(src, seg, n)
kernel_name = 'mk_seq_preln_d1_jaxref_r4_368b89'

def setup_inputs(seed: int=0):
    np.random.seed(seed)
    _w = jnp.asarray

    def _L0_attn_setup():
        import jax, jax.numpy as jnp
        import numpy as np
        D_MODEL, D_INNER, D_STATE, D_CONV, DT_RANK = (256, 512, 16, 4, 64)
        BATCH, SEQLEN = (4, 512)

        def _silu(x):
            return x * jax.nn.sigmoid(x)

        def _mamba_forward(hidden_states, in_proj_w, conv_w, conv_b, x_proj_w, dt_proj_w, dt_proj_b, A_log, D, out_proj_w):
            B, L, _ = hidden_states.shape
            d_inner, d_conv = conv_w.shape
            d_state = A_log.shape[1]
            dt_rank = dt_proj_w.shape[1]
            xz = jnp.einsum('bld,ed->ble', hidden_states, in_proj_w)
            x, z = (xz[..., :d_inner], xz[..., d_inner:])
            x_pad = jnp.pad(x, ((0, 0), (d_conv - 1, 0), (0, 0)))
            x_conv = sum((x_pad[:, w:w + L, :] * conv_w[:, w] for w in range(d_conv))) + conv_b
            x_conv = _silu(x_conv)
            x_dbl = jnp.einsum('bld,ed->ble', x_conv, x_proj_w)
            dt_in = x_dbl[..., :dt_rank]
            Bv = x_dbl[..., dt_rank:dt_rank + d_state]
            Cv = x_dbl[..., dt_rank + d_state:]
            delta = jax.nn.softplus(jnp.einsum('blr,dr->bld', dt_in, dt_proj_w) + dt_proj_b)
            A = -jnp.exp(A_log)

            def step(h, inp):
                d_t, B_t, C_t, u_t = inp
                dA = jnp.exp(d_t[:, :, None] * A)
                h = h * dA + (d_t * u_t)[:, :, None] * B_t[:, None, :]
                y = jnp.einsum('bdn,bn->bd', h, C_t)
                return (h, y)
            h0 = jnp.zeros((B, d_inner, d_state), dtype=hidden_states.dtype)
            xs = (jnp.swapaxes(delta, 0, 1), jnp.swapaxes(Bv, 0, 1), jnp.swapaxes(Cv, 0, 1), jnp.swapaxes(x_conv, 0, 1))
            _, ys = jax.lax.scan(step, h0, xs)
            y = jnp.swapaxes(ys, 0, 1) + x_conv * D
            y = y * _silu(z)
            return jnp.einsum('bld,md->blm', y, out_proj_w)
        key = jax.random.key(seed)
        ks = jax.random.split(key, 10)

        def n(k, shape, scale=1.0):
            return jax.random.normal(k, shape, dtype=jnp.float32) * scale
        A_log = jnp.log(jax.random.uniform(ks[7], (D_INNER, D_STATE), dtype=jnp.float32, minval=0.5, maxval=float(D_STATE)))
        return {'hidden_states': n(ks[0], (BATCH, SEQLEN, D_MODEL)), 'in_proj_w': n(ks[1], (2 * D_INNER, D_MODEL), D_MODEL ** (-0.5)), 'conv_w': n(ks[2], (D_INNER, D_CONV), D_CONV ** (-0.5)), 'conv_b': n(ks[3], (D_INNER,), 0.1), 'x_proj_w': n(ks[4], (DT_RANK + 2 * D_STATE, D_INNER), D_INNER ** (-0.5)), 'dt_proj_w': n(ks[5], (D_INNER, DT_RANK), DT_RANK ** (-0.5)), 'dt_proj_b': n(ks[6], (D_INNER,), 0.5), 'A_log': A_log, 'D': jnp.ones((D_INNER,), dtype=jnp.float32), 'out_proj_w': n(ks[8], (D_MODEL, D_INNER), D_INNER ** (-0.5))}
    _L0_attn_in = _L0_attn_setup()

    def _L0_ffn_setup():
        import jax, jax.numpy as jnp
        import numpy as np
        S_LEN, BATCH, HIDDEN = (512, 2, 256)
        N_HEADS, N_KV = (16, 8)
        N_EXP, TOP_K, CAP_F = (8, 2, 1.25)
        FFN = 1024
        HEAD_DIM = HIDDEN // N_HEADS
        Q_PER_KV = N_HEADS // N_KV
        EPS = 1e-05
        NEG = -1000000000.0

        def _ln(x, w, b):
            mu = jnp.mean(x, -1, keepdims=True)
            var = jnp.var(x, -1, keepdims=True)
            return (x - mu) * jax.lax.rsqrt(var + EPS) * w + b

        def _forward(hidden_states, ln1_weight, ln1_bias, ln2_weight, ln2_bias, qkv_weight, proj_weight, router_weight, moe_w1, moe_w2):
            S, B, H = hidden_states.shape
            ln1 = _ln(hidden_states, ln1_weight, ln1_bias)
            qkv = (ln1 @ qkv_weight.T).reshape(S, B, N_KV, (Q_PER_KV + 2) * HEAD_DIM)
            q_dim = Q_PER_KV * HEAD_DIM
            q = qkv[..., :q_dim].reshape(S, B, N_HEADS, HEAD_DIM)
            k = jnp.repeat(qkv[..., q_dim:q_dim + HEAD_DIM], Q_PER_KV, axis=2)
            v = jnp.repeat(qkv[..., q_dim + HEAD_DIM:], Q_PER_KV, axis=2)
            scores = jnp.einsum('sbhd,tbhd->bhst', q, k) / jnp.sqrt(jnp.float32(HEAD_DIM))
            causal = jnp.tril(jnp.ones((S, S), bool))
            attn = jax.nn.softmax(jnp.where(causal[None, None], scores, NEG), axis=-1)
            attn_out = jnp.einsum('bhst,tbhd->sbhd', attn, v).reshape(S, B, H)
            hidden_after_attn = hidden_states + attn_out @ proj_weight.T
            x = _ln(hidden_after_attn, ln2_weight, ln2_bias).reshape(-1, H)
            N = S * B
            probs = jax.nn.softmax(x.astype(jnp.float32) @ router_weight, axis=-1)
            top_p, top_i = jax.lax.top_k(probs, TOP_K)
            top_p = top_p / jnp.sum(top_p, -1, keepdims=True)
            flat_exp = top_i.reshape(-1)
            order = jnp.argsort(flat_exp)
            sorted_exp = flat_exp[order]
            counts = jnp.bincount(sorted_exp, length=N_EXP)
            offsets = jnp.concatenate([jnp.zeros((1,), counts.dtype), jnp.cumsum(counts)])
            within = jnp.arange(N * TOP_K) - offsets[sorted_exp]
            cap = int(np.ceil(N * TOP_K / N_EXP * CAP_F))
            keep = within < cap
            slot = jnp.where(keep, sorted_exp * cap + within, N_EXP * cap)
            tok_id = order // TOP_K
            padded_tokens = jnp.zeros((N_EXP * cap + 1, H), x.dtype).at[slot].set(x[tok_id])[:-1]
            padded_probs = jnp.zeros((N_EXP * cap + 1,), jnp.float32).at[slot].set(top_p.reshape(-1)[order])[:-1]
            padded_ids = jnp.zeros((N_EXP * cap + 1,), jnp.int32).at[slot].set(tok_id.astype(jnp.int32))[:-1]
            exp_in = padded_tokens.reshape(N_EXP, cap, H)
            act = jax.nn.gelu(jnp.einsum('ech,ehf->ecf', exp_in, moe_w1), approximate=False)
            exp_out = jnp.einsum('ecf,efh->ech', act, moe_w2).reshape(N_EXP * cap, H)
            weighted = exp_out * padded_probs[:, None].astype(exp_out.dtype)
            moe = jnp.zeros((N, H), exp_out.dtype).at[padded_ids].add(weighted)
            return hidden_after_attn + moe.reshape(S, B, H)
        ks = jax.random.split(jax.random.key(seed), 6)
        qkv_out = N_KV * (Q_PER_KV + 2) * HEAD_DIM
        sc = 0.02
        return {'hidden_states': jax.random.normal(ks[0], (S_LEN, BATCH, HIDDEN), jnp.float32), 'ln1_weight': jnp.ones((HIDDEN,), jnp.float32), 'ln1_bias': jnp.zeros((HIDDEN,), jnp.float32), 'ln2_weight': jnp.ones((HIDDEN,), jnp.float32), 'ln2_bias': jnp.zeros((HIDDEN,), jnp.float32), 'qkv_weight': jax.random.normal(ks[1], (qkv_out, HIDDEN), jnp.float32) * sc, 'proj_weight': jax.random.normal(ks[2], (HIDDEN, HIDDEN), jnp.float32) * sc, 'router_weight': jax.random.normal(ks[3], (HIDDEN, N_EXP), jnp.float32) * sc, 'moe_w1': jax.random.normal(ks[4], (N_EXP, HIDDEN, FFN), jnp.float32) * sc, 'moe_w2': jax.random.normal(ks[5], (N_EXP, FFN, HIDDEN), jnp.float32) * sc}
    _L0_ffn_in = _L0_ffn_setup()
    _d = {'L0_attn_hidden_states': _L0_attn_in['hidden_states'], 'L0_attn_in_proj_w': _L0_attn_in['in_proj_w'], 'L0_attn_conv_w': _L0_attn_in['conv_w'], 'L0_attn_conv_b': _L0_attn_in['conv_b'], 'L0_attn_x_proj_w': _L0_attn_in['x_proj_w'], 'L0_attn_dt_proj_w': _L0_attn_in['dt_proj_w'], 'L0_attn_dt_proj_b': _L0_attn_in['dt_proj_b'], 'L0_attn_A_log': _L0_attn_in['A_log'], 'L0_attn_D': _L0_attn_in['D'], 'L0_attn_out_proj_w': _L0_attn_in['out_proj_w'], 'L0_ffn_ln1_weight': _L0_ffn_in['ln1_weight'], 'L0_ffn_ln1_bias': _L0_ffn_in['ln1_bias'], 'L0_ffn_ln2_weight': _L0_ffn_in['ln2_weight'], 'L0_ffn_ln2_bias': _L0_ffn_in['ln2_bias'], 'L0_ffn_qkv_weight': _L0_ffn_in['qkv_weight'], 'L0_ffn_proj_weight': _L0_ffn_in['proj_weight'], 'L0_ffn_router_weight': _L0_ffn_in['router_weight'], 'L0_ffn_moe_w1': _L0_ffn_in['moe_w1'], 'L0_ffn_moe_w2': _L0_ffn_in['moe_w2']}
    _x0 = _d['L0_attn_hidden_states']
    _d['L0_attn_hidden_states'] = jax.random.normal(jax.random.fold_in(jax.random.key(seed), 1), (16, 1024, 256), dtype=_x0.dtype)
    del _x0
    return _d

def reference(L0_attn_hidden_states, L0_attn_in_proj_w, L0_attn_conv_w, L0_attn_conv_b, L0_attn_x_proj_w, L0_attn_dt_proj_w, L0_attn_dt_proj_b, L0_attn_A_log, L0_attn_D, L0_attn_out_proj_w, L0_ffn_ln1_weight, L0_ffn_ln1_bias, L0_ffn_ln2_weight, L0_ffn_ln2_bias, L0_ffn_qkv_weight, L0_ffn_proj_weight, L0_ffn_router_weight, L0_ffn_moe_w1, L0_ffn_moe_w2):

    def _L0_attn_ref(hidden_states, in_proj_w, conv_w, conv_b, x_proj_w, dt_proj_w, dt_proj_b, A_log, D, out_proj_w):
        import jax, jax.numpy as jnp
        import numpy as np
        D_MODEL, D_INNER, D_STATE, D_CONV, DT_RANK = (256, 512, 16, 4, 64)
        BATCH, SEQLEN = (4, 512)

        def _silu(x):
            return x * jax.nn.sigmoid(x)

        def _mamba_forward(hidden_states, in_proj_w, conv_w, conv_b, x_proj_w, dt_proj_w, dt_proj_b, A_log, D, out_proj_w):
            B, L, _ = hidden_states.shape
            d_inner, d_conv = conv_w.shape
            d_state = A_log.shape[1]
            dt_rank = dt_proj_w.shape[1]
            xz = jnp.einsum('bld,ed->ble', hidden_states, in_proj_w)
            x, z = (xz[..., :d_inner], xz[..., d_inner:])
            x_pad = jnp.pad(x, ((0, 0), (d_conv - 1, 0), (0, 0)))
            x_conv = sum((x_pad[:, w:w + L, :] * conv_w[:, w] for w in range(d_conv))) + conv_b
            x_conv = _silu(x_conv)
            x_dbl = jnp.einsum('bld,ed->ble', x_conv, x_proj_w)
            dt_in = x_dbl[..., :dt_rank]
            Bv = x_dbl[..., dt_rank:dt_rank + d_state]
            Cv = x_dbl[..., dt_rank + d_state:]
            delta = jax.nn.softplus(jnp.einsum('blr,dr->bld', dt_in, dt_proj_w) + dt_proj_b)
            A = -jnp.exp(A_log)

            def step(h, inp):
                d_t, B_t, C_t, u_t = inp
                dA = jnp.exp(d_t[:, :, None] * A)
                h = h * dA + (d_t * u_t)[:, :, None] * B_t[:, None, :]
                y = jnp.einsum('bdn,bn->bd', h, C_t)
                return (h, y)
            h0 = jnp.zeros((B, d_inner, d_state), dtype=hidden_states.dtype)
            xs = (jnp.swapaxes(delta, 0, 1), jnp.swapaxes(Bv, 0, 1), jnp.swapaxes(Cv, 0, 1), jnp.swapaxes(x_conv, 0, 1))
            _, ys = jax.lax.scan(step, h0, xs)
            y = jnp.swapaxes(ys, 0, 1) + x_conv * D
            y = y * _silu(z)
            return jnp.einsum('bld,md->blm', y, out_proj_w)
        return _mamba_forward(hidden_states, in_proj_w, conv_w, conv_b, x_proj_w, dt_proj_w, dt_proj_b, A_log, D, out_proj_w)

    def _L0_ffn_ref(hidden_states, ln1_weight, ln1_bias, ln2_weight, ln2_bias, qkv_weight, proj_weight, router_weight, moe_w1, moe_w2):
        import jax, jax.numpy as jnp
        import numpy as np
        S_LEN, BATCH, HIDDEN = (512, 2, 256)
        N_HEADS, N_KV = (16, 8)
        N_EXP, TOP_K, CAP_F = (8, 2, 1.25)
        FFN = 1024
        HEAD_DIM = HIDDEN // N_HEADS
        Q_PER_KV = N_HEADS // N_KV
        EPS = 1e-05
        NEG = -1000000000.0

        def _ln(x, w, b):
            mu = jnp.mean(x, -1, keepdims=True)
            var = jnp.var(x, -1, keepdims=True)
            return (x - mu) * jax.lax.rsqrt(var + EPS) * w + b

        def _forward(hidden_states, ln1_weight, ln1_bias, ln2_weight, ln2_bias, qkv_weight, proj_weight, router_weight, moe_w1, moe_w2):
            S, B, H = hidden_states.shape
            ln1 = _ln(hidden_states, ln1_weight, ln1_bias)
            qkv = (ln1 @ qkv_weight.T).reshape(S, B, N_KV, (Q_PER_KV + 2) * HEAD_DIM)
            q_dim = Q_PER_KV * HEAD_DIM
            q = qkv[..., :q_dim].reshape(S, B, N_HEADS, HEAD_DIM)
            k = jnp.repeat(qkv[..., q_dim:q_dim + HEAD_DIM], Q_PER_KV, axis=2)
            v = jnp.repeat(qkv[..., q_dim + HEAD_DIM:], Q_PER_KV, axis=2)
            scores = jnp.einsum('sbhd,tbhd->bhst', q, k) / jnp.sqrt(jnp.float32(HEAD_DIM))
            causal = jnp.tril(jnp.ones((S, S), bool))
            attn = jax.nn.softmax(jnp.where(causal[None, None], scores, NEG), axis=-1)
            attn_out = jnp.einsum('bhst,tbhd->sbhd', attn, v).reshape(S, B, H)
            hidden_after_attn = hidden_states + attn_out @ proj_weight.T
            x = _ln(hidden_after_attn, ln2_weight, ln2_bias).reshape(-1, H)
            N = S * B
            probs = jax.nn.softmax(x.astype(jnp.float32) @ router_weight, axis=-1)
            top_p, top_i = jax.lax.top_k(probs, TOP_K)
            top_p = top_p / jnp.sum(top_p, -1, keepdims=True)
            flat_exp = top_i.reshape(-1)
            order = jnp.argsort(flat_exp)
            sorted_exp = flat_exp[order]
            counts = jnp.bincount(sorted_exp, length=N_EXP)
            offsets = jnp.concatenate([jnp.zeros((1,), counts.dtype), jnp.cumsum(counts)])
            within = jnp.arange(N * TOP_K) - offsets[sorted_exp]
            cap = int(np.ceil(N * TOP_K / N_EXP * CAP_F))
            keep = within < cap
            slot = jnp.where(keep, sorted_exp * cap + within, N_EXP * cap)
            tok_id = order // TOP_K
            padded_tokens = jnp.zeros((N_EXP * cap + 1, H), x.dtype).at[slot].set(x[tok_id])[:-1]
            padded_probs = jnp.zeros((N_EXP * cap + 1,), jnp.float32).at[slot].set(top_p.reshape(-1)[order])[:-1]
            padded_ids = jnp.zeros((N_EXP * cap + 1,), jnp.int32).at[slot].set(tok_id.astype(jnp.int32))[:-1]
            exp_in = padded_tokens.reshape(N_EXP, cap, H)
            act = jax.nn.gelu(jnp.einsum('ech,ehf->ecf', exp_in, moe_w1), approximate=False)
            exp_out = jnp.einsum('ecf,efh->ech', act, moe_w2).reshape(N_EXP * cap, H)
            weighted = exp_out * padded_probs[:, None].astype(exp_out.dtype)
            moe = jnp.zeros((N, H), exp_out.dtype).at[padded_ids].add(weighted)
            return hidden_after_attn + moe.reshape(S, B, H)
        return _forward(hidden_states, ln1_weight, ln1_bias, ln2_weight, ln2_bias, qkv_weight, proj_weight, router_weight, moe_w1, moe_w2)
    x = L0_attn_hidden_states
    x = x + _L0_attn_ref(_layernorm(x, axis=-1), L0_attn_in_proj_w, L0_attn_conv_w, L0_attn_conv_b, L0_attn_x_proj_w, L0_attn_dt_proj_w, L0_attn_dt_proj_b, L0_attn_A_log, L0_attn_D, L0_attn_out_proj_w)
    x = x + _L0_ffn_ref(_layernorm(x, axis=-1), L0_ffn_ln1_weight, L0_ffn_ln1_bias, L0_ffn_ln2_weight, L0_ffn_ln2_bias, L0_ffn_qkv_weight, L0_ffn_proj_weight, L0_ffn_router_weight, L0_ffn_moe_w1, L0_ffn_moe_w2)
    return x

_drawn_inputs = setup_inputs


def setup_inputs(seed=0):
    import zlib

    import numpy as np

    out = dict(_drawn_inputs(seed))
    spreads = {'L0_attn_D': (1.0, 0.2),
     'L0_ffn_ln1_weight': (1.0, 0.6),
     'L0_ffn_ln1_bias': (0.0, 0.8),
     'L0_ffn_ln2_weight': (1.0, 0.6),
     'L0_ffn_ln2_bias': (0.0, 0.537)}
    factors = {}
    for name, (base, spread) in spreads.items():
        noise = np.random.default_rng([zlib.crc32(name.encode()), seed]).standard_normal(out[name].shape)
        drawn = base * np.exp(spread * noise) if base else spread * noise
        out[name] = jnp.asarray(drawn.astype(out[name].dtype))
    for name, factor in factors.items():
        out[name] = (out[name] * factor).astype(out[name].dtype)
    return out
```

```python
from contextlib import ExitStack

import concourse.bass as bass
from concourse import mybir

F32 = mybir.dt.float32
BF16 = mybir.dt.bfloat16
I32 = mybir.dt.int32
ALU = mybir.AluOpType
ACT = mybir.ActivationFunctionType
AXX = mybir.AxisListType.X

P = 128
S, L, H = 16, 1024, 256
TOKENS = S * L
DI, NS, R, TAPS = 512, 16, 64, 4
CH = DI // P
KH = H // P
T = 512
TB = T // P
HALVES = L // T
EPS = 1e-5
HEADS, KV, HD = 16, 8, 16
EXPERTS, TOPK, FFN = 8, 2, 1024
CAP = 5120
SLOTS = EXPERTS * CAP


class Allocator:

    def __init__(self, nc, ctx, prefix):
        self.nc, self.ctx, self.prefix = nc, ctx, prefix

    def sb(self, name, shape, dtype=F32):
        return self.ctx.enter_context(self.nc.sbuf_tensor(self.prefix + name, shape, dtype))

    def ps(self, name, shape, dtype=F32):
        return self.ctx.enter_context(self.nc.psum_tensor(self.prefix + name, shape, dtype))

    def sem(self, name):
        return self.ctx.enter_context(self.nc.semaphore(self.prefix + name))


def count(block, per_block, done):
    b, half = block
    return b * (HALVES * per_block) + (half * per_block + done)


def wait(eng, sem, value):
    if isinstance(value, int) and value <= 0:
        return
    eng.wait_ge(sem, value)


def wait_apart(eng, sem, value, passed):
    if isinstance(value, int) and value <= 0:
        return
    eng.wait_ge(sem, value)
    eng.sem_inc(passed, 1)


def mamba_stage(nc, x, w, x1):
    SLOT = {2: ("y", 0), 3: ("y", 1), 4: ("y", 2), 5: ("y", 3), 6: ("xnT", 0), 7: ("xnT", 1),
            8: ("out", 0), 9: ("out", 1), 10: ("x", 0), 11: ("x", 1), 12: ("x", 2), 13: ("x", 3),
            14: ("conv", 0), 15: ("conv", 1), 16: ("conv", 2), 17: ("conv", 3), 18: ("z", 0),
            19: ("dbl", 0), 20: ("z", 1), 21: ("z", 2), 22: ("z", 3), 23: ("dt", 0), 24: ("dt", 1),
            25: ("dt", 2), 26: ("dt", 3), 27: ("C", 0), 28: ("skip", 0), 29: ("skip", 1),
            30: ("skip", 2), 31: ("skip", 3)}
    VECTOR_KINDS = ("y", "out")
    gate_slots = [v for v in sorted(SLOT) if SLOT[v][0] in VECTOR_KINDS]
    prep_slots = [v for v in sorted(SLOT) if SLOT[v][0] not in VECTOR_KINDS]
    GATES, PREPS = len(gate_slots), len(prep_slots)

    def prep_done(kind, i):
        return 1 + [SLOT[v] for v in prep_slots].index((kind, i))

    with ExitStack() as ctx:
        al = Allocator(nc, ctx, "m_")
        sb, sem = al.sb, al.sem
        w_in = sb("w_in", [P, KH, 2 * DI])
        w_x = sb("w_x", [P, CH, P])
        w_dt = sb("w_dt", [R, DI])
        w_out = sb("w_out", [P, CH, H])
        a_log = sb("a_log", [P, CH, NS])
        a_neg = sb("a_neg", [P, CH, NS])
        conv_w = sb("conv_w", [P, CH, TAPS])
        vecs = sb("vecs", [P, 3, CH])
        half_bias = sb("half_bias", [P, CH])
        ident = sb("ident", [P, P])
        tap_diag = sb("tap_diag", [P, CH, TAPS, P])
        skip_diag = sb("skip_diag", [P, CH, P])
        pick = sb("pick", [R + NS, NS, P])
        xin = sb("xin", [P, TB, H])
        stats = sb("stats", [P, TB, 6])
        moments = sb("moments", [P, TB, 2])
        rstd = sb("rstd", [P, TB])
        minus_half = sb("minus_half", [P, TB])
        eps = sb("eps", [P, TB])
        xn = sb("xn", [P, TB, H])
        xnT = sb("xnT", [P, KH, T])
        xpad = sb("xpad", [P, CH, TAPS - 1 + T])
        tanh = sb("tanh", [P, 2, T])
        hlf = sb("hlf", [P, 2, T])
        xc = sb("xc", [P, CH, T])
        dbl = sb("dbl", [P, 2, T])
        sp_e = sb("sp_e", [P, CH, T])
        sp_r = sb("sp_r", [P, CH, T])
        delta = sb("delta", [P, 2, CH, T])
        du = sb("du", [P, 2, CH, T])
        zs = sb("zs", [P, 2, CH, T])
        cT = sb("cT", [P, 2, TB, NS])
        bb = sb("bb", [P, 2, T])
        dbu = sb("dbu", [P, 2, CH, T])
        h = sb("h", [P, 2, CH, T])
        h_end = sb("h_end", [P, NS, CH])
        acc = sb("acc", [P, 2, TB, DI])
        y = sb("y", [P, CH, T])
        xres = sb("xres", [P, TB, H])
        decay = al.ps("decay", [P, 2, T])
        hT = al.ps("hT", [P, 2, DI])
        bcast = al.ps("bcast", [P, 2, T])
        slot_bank = al.ps("slot", [P, 2, T])

        s_weights = sem("weights")
        s_const = sem("const")
        s_a = sem("a")
        s_diag = sem("diag")
        dve_passed, sp_passed = sem("dve_passed"), sem("sp_passed")
        x_loaded = sem("x_loaded")
        xres_loaded = sem("xres_loaded")
        x1_stored = sem("x1_stored")
        stats_done = sem("stats_done")
        rstd_done = sem("rstd_done")
        ln_done = sem("ln_done")
        prep_made = sem("prep_made")
        prep_taken = sem("prep_taken")
        gate_made = sem("gate_made")
        gate_taken = sem("gate_taken")
        halo_done = sem("halo_done")
        tanh_done = sem("tanh_done")
        silu_done = sem("silu_done")
        soft_done = sem("soft_done")
        delta_done = sem("delta_done")
        du_done = sem("du_done")
        bcast_made = sem("bcast_made")
        bb_done = sem("bb_done")
        dbu_done = sem("dbu_done")
        decay_done = sem("decay_done")
        scan_done = sem("scan_done")
        hT_done = sem("hT_done")
        sum_done = sem("sum_done")
        end_saved = sem("end_saved")

        x_blocks = x.rearrange("s (h j p) m -> s h p j m", h=HALVES, p=P)
        x1_blocks = x1.rearrange("s (h j p) m -> s h p j m", h=HALVES, p=P)

        block = ctx.enter_context(nc.Block())

        def before(q):
            return (q[0], q[1] - 1) if q[1] else (q[0] - 1, HALVES - 1)

        def after(q):
            return (q[0], q[1] + 1) if q[1] < HALVES - 1 else (q[0] + 1, 0)

        def first(q):
            return isinstance(q[0], int) and q[0] == 0 and q[1] == 0

        def sequences(eng, body):
            body(0, False)
            with eng.Fori(1, S - 1) as b:
                body(b, False)
            body(S - 1, True)

        @block.sync
        def _(sp):
            def wait_then_address(sem_, value):
                wait_apart(sp, sem_, value, sp_passed)

            def load_x(q):
                if not first(q):
                    wait_then_address(ln_done, count(q, 1, 0))
                sp.dma_start(xin[:], x_blocks[q[0], q[1]]).then_inc(x_loaded, 16)

            def move(q, last):
                if not last:
                    load_x(after(q))
                if not first(q):
                    g = before(q)
                    wait_then_address(x1_stored, count(g, 16, 0))
                    sp.dma_start(xres[:], x_blocks[g[0], g[1]]).then_inc(xres_loaded, 16)
                    wait_then_address(gate_taken, count(g, GATES, GATES))
                    sp.dma_start(x1_blocks[g[0], g[1]], xres[:]).then_inc(x1_stored, 16)

            load_x((0, 0))
            for dst, src in ((w_in[:], w["in_T"].rearrange("(k p) e -> p k e", p=P)),
                             (w_dt[:], w["dt_T"]),
                             (w_out[:], w["out_T"].rearrange("(c p) m -> p c m", p=P)),
                             (a_log[:], w["A_log"].rearrange("(c p) n -> p c n", p=P)),
                             (conv_w[:], w["conv_w"].rearrange("(c p) k -> p c k", p=P)),
                             (vecs[:], w["vecs"].rearrange("v p c -> p v c"))):
                sp.dma_start(dst, src).then_inc(s_weights, 16)
            sp.wait_ge(s_const, 5)
            w_xT = w["x_T"].rearrange("(c p) e -> p c e", p=P)
            sp.dma_start(w_x[:, :, 0:R + NS], w_xT[:, :, 0:R + NS]).then_inc(s_weights, 16)
            sp.dma_start(w_x[:, :, 96:96 + NS], w_xT[:, :, R + NS:R + 2 * NS]).then_inc(s_weights, 16)

            def body(b, last):
                for half in range(HALVES):
                    move((b, half), last and half == HALVES - 1)
            sequences(sp, body)
            g = (S - 1, HALVES - 1)
            sp.wait_ge(x1_stored, count(g, 16, 0))
            sp.dma_start(xres[:], x_blocks[g[0], g[1]]).then_inc(xres_loaded, 16)
            sp.wait_ge(gate_taken, count(g, GATES, GATES))
            sp.dma_start(x1_blocks[g[0], g[1]], xres[:]).then_inc(x1_stored, 16)
            sp.wait_ge(x1_stored, 16 * S * HALVES)

        @block.gpsimd
        def _(pool):
            nc.gpsimd.memset(minus_half[:], -0.5).then_inc(s_const, 1)
            nc.gpsimd.memset(eps[:], EPS).then_inc(s_const, 1)
            nc.gpsimd.memset(ident[:], 0.0).then_inc(s_const, 1)
            nc.gpsimd.memset(pick[:], 0.0).then_inc(s_const, 1)
            nc.gpsimd.memset(w_x[:], 0.0).then_inc(s_const, 1)
            pool.wait_ge(s_const, 5)
            nc.gpsimd.affine_select(out=ident[:], in_=ident[:], compare_op=ALU.not_equal, fill=1.0,
                                    base=0, pattern=[[-1, P]], channel_multiplier=1).then_inc(s_const, 1)
            nc.gpsimd.affine_select(out=pick[:], in_=pick[:], compare_op=ALU.not_equal, fill=1.0,
                                    base=-R, pattern=[[-1, NS], [0, P]], channel_multiplier=1).then_inc(s_const, 1)

            def inverse_deviation(q):
                wait(pool, stats_done, count(q, 2, 2))
                nc.gpsimd.tensor_tensor(rstd[:], moments[:, :, 1], eps[:], ALU.add).then_inc(rstd_done, 1)
                wait(pool, rstd_done, count(q, 2, 1))
                nc.gpsimd.tensor_tensor(rstd[:], rstd[:], minus_half[:], ALU.pow).then_inc(rstd_done, 1)

            inverse_deviation((0, 0))

            def body(b, last):
                for half in range(HALVES):
                    q = (b, half)
                    wait(pool, du_done, count(q, 1, 1))
                    for n in range(NS):
                        wait(pool, bb_done, count(q, NS, n + 1))
                        wait(pool, scan_done, count(q, 4 * NS, 4 * (n - 1)))
                        nc.gpsimd.tensor_tensor(
                            dbu[:, n % 2], du[:, half],
                            bb[:, n % 2].unsqueeze(1).to_broadcast([P, CH, T]),
                            ALU.mult).then_inc(dbu_done, 1)
                        if n == 1 and not (last and half == HALVES - 1):
                            inverse_deviation(after(q))
            sequences(pool, body)

        @block.scalar
        def _(act):
            act.wait_ge(s_weights, 16 * 8)
            act.wait_ge(s_const, 7)
            nc.scalar.activation(a_neg[:], a_log[:], ACT.Exp).then_inc(s_a, 1)
            nc.scalar.mul(half_bias[:], vecs[:, 0, :], 0.5).then_inc(s_a, 1)
            act.wait_ge(s_a, 1)
            nc.scalar.mul(a_neg[:], a_neg[:], -1.0).then_inc(s_a, 1)
            act.wait_ge(s_a, 3)

            def take(q, v):
                kind, i = SLOT[v]
                bank = slot_bank[:, v % 2]
                r = q[1]
                wait(act, prep_made, count(q, PREPS, prep_done(kind, i)))
                if kind == "xnT":
                    ins = nc.scalar.copy(xnT[:, i], bank)
                elif kind == "x":
                    if i == 0:
                        wait(act, prep_made, count(before(q), PREPS, prep_done("conv", CH - 1)))
                        wait(act, prep_taken, count(before(q), PREPS, prep_done("x", CH - 1)))
                        if r:
                            nc.scalar.copy(xpad[:, :, 0:TAPS - 1], xpad[:, :, T:T + TAPS - 1]).then_inc(halo_done, 1)
                        else:
                            nc.scalar.mul(xpad[:, :, 0:TAPS - 1], ident[:, 0:CH * (TAPS - 1)].rearrange(
                                "p (c k) -> p c k", c=CH), 0.0).then_inc(halo_done, 1)
                        wait(act, halo_done, count(q, 1, 1))
                    ins = nc.scalar.copy(xpad[:, i, TAPS - 1:], bank)
                elif kind in ("conv", "z"):
                    k = i + (CH if kind == "z" else 0)
                    wait(act, silu_done, count(q, 2 * CH, k - 1))
                    bias = half_bias[:, i:i + 1] if kind == "conv" else 0.0
                    nc.scalar.activation(tanh[:, k % 2], bank, ACT.Tanh, scale=0.5, bias=bias)
                    ins = nc.scalar.activation(hlf[:, k % 2], bank, ACT.Identity, scale=0.5, bias=bias)
                elif kind == "dbl":
                    wait(act, bcast_made, count(before(before(q)), NS, NS))
                    ins = nc.scalar.copy(dbl[:, r], bank)
                elif kind == "dt":
                    if i == 0:
                        wait(act, delta_done, count(q, 1, 0))
                    nc.scalar.activation(sp_e[:, i], bank, ACT.Abs, bias=vecs[:, 1, i:i + 1])
                    ins = nc.scalar.activation(sp_r[:, i], bank, ACT.Relu, bias=vecs[:, 1, i:i + 1])
                elif kind == "C":
                    wait(act, sum_done, count(before(before(q)), 4 * NS, 4 * NS))
                    ins = nc.scalar.copy(cT[:, r], bank.rearrange("p (j e) -> p j e", j=TB)[:, :, 96:96 + NS])
                elif kind == "skip":
                    wait(act, gate_made, count(before(before(q)), GATES, CH))
                    ins = nc.scalar.copy(acc[:, r, i], bank)
                ins.then_inc(prep_taken, 1)

            def softplus(q):
                wait(act, prep_taken, count(q, PREPS, prep_done("dt", CH - 1)))
                nc.scalar.activation(sp_e[:], sp_e[:], ACT.Exp, scale=-1.0).then_inc(soft_done, 1)
                wait(act, soft_done, count(q, 2, 1))
                nc.scalar.activation(sp_e[:], sp_e[:], ACT.Ln, bias=1.0).then_inc(soft_done, 1)

            def prepare(q, v):
                if v in prep_slots:
                    take(q, v)
                if v == prep_slots[[SLOT[u] for u in prep_slots].index(("C", 0))]:
                    softplus(q)

            for v in range(32):
                prepare((0, 0), v)

            def copy_b(q, n):
                wait(act, bcast_made, count(q, NS, n + 1))
                wait(act, dbu_done, count(q, NS, n - 1))
                nc.scalar.copy(bb[:, n % 2], bcast[:, n % 2]).then_inc(bb_done, 1)

            def scan_block(q, last):
                r = q[1]
                wait(act, delta_done, count(q, 1, 1))
                for n in range(NS):
                    copy_b(q, n)
                    for c in range(CH):
                        wait(act, scan_done, count(q, 4 * NS, 4 * n + c - 1))
                        nc.scalar.activation(decay[:, c % 2], delta[:, r, c], ACT.Exp,
                                             scale=a_neg[:, c, n:n + 1]).then_inc(decay_done, 1)
                        if c % 2 and not last and 2 * n + c // 2 >= 1:
                            prepare(after(q), 2 * n + c // 2 - 1)
                if not last:
                    prepare(after(q), 31)

            def body(b, last):
                for half in range(HALVES):
                    scan_block((b, half), last and half == HALVES - 1)
            sequences(act, body)

        @block.vector
        def _(dve):
            dve.wait_ge(s_weights, 16 * 8)
            dve.wait_ge(s_const, 7)
            for c in range(CH):
                for k in range(TAPS):
                    nc.vector.tensor_scalar(tap_diag[:, c, k], ident[:], conv_w[:, c, k:k + 1], None, ALU.mult)
                ins = nc.vector.tensor_scalar(skip_diag[:, c], ident[:], vecs[:, 2, c:c + 1], None, ALU.mult)
            ins.then_inc(s_diag, 1)

            def statistics(q):
                wait(dve, x_loaded, count(q, 16, 16))
                for j in range(TB):
                    ins = nc.vector.bn_stats(stats[:, j], xin[:, j])
                ins.then_inc(stats_done, 1)
                wait_apart(dve, stats_done, count(q, 2, 1), dve_passed)
                for j in range(TB):
                    ins = nc.vector.bn_aggr(moments[:, j], stats[:, j])
                ins.then_inc(stats_done, 1)

            def normalise(q, part):
                if part == 0:
                    wait(dve, rstd_done, count(q, 2, 2))
                    wait(dve, prep_made, count(before(q), PREPS, prep_done("xnT", 1)))
                for j in range(2 * part, 2 * part + 2):
                    ins = nc.vector.tensor_scalar(xn[:, j], xin[:, j], moments[:, j, 0:1], rstd[:, j:j + 1],
                                                  ALU.subtract, ALU.mult)
                if part:
                    ins.then_inc(ln_done, 1)

            def silu(q, v):
                kind, i = SLOT[v]
                k = i + (CH if kind == "z" else 0)
                wait(dve, prep_taken, count(q, PREPS, prep_done(kind, i)))
                if kind == "conv" and i == 0:
                    wait(dve, prep_made, count(before(q), PREPS, prep_done("skip", TB - 1)))
                if kind == "z" and i == 0:
                    wait(dve, gate_taken, count(before(before(q)), GATES, CH))
                out = xc[:, i] if kind == "conv" else zs[:, q[1], i]
                nc.vector.scalar_tensor_tensor(out=out, in0=tanh[:, k % 2], scalar=1.0, in1=hlf[:, k % 2],
                                               op0=ALU.add, op1=ALU.mult).then_inc(silu_done, 1)

            def gate(q, v):
                kind, i = SLOT[v]
                wait(dve, gate_made, count(q, GATES, 1 + gate_slots.index(v)))
                bank = slot_bank[:, v % 2]
                if kind == "y":
                    if i == 0:
                        wait(dve, gate_made, count(before(q), GATES, GATES))
                    nc.vector.tensor_tensor(y[:, i], bank, zs[:, q[1], i], ALU.mult).then_inc(gate_taken, 1)
                else:
                    if i == 0:
                        wait(dve, xres_loaded, count(q, 16, 16))
                    nc.vector.tensor_tensor(xres[:, 2 * i:2 * i + 2], bank.rearrange("p (j m) -> p j m", j=2),
                                            xres[:, 2 * i:2 * i + 2], ALU.add).then_inc(gate_taken, 1)

            def side_work(q, v, gates, preps):
                if v == 0 and preps:
                    statistics(after(q))
                if v in (4, 5) and preps:
                    normalise(after(q), v - 4)
                if v - 1 in gate_slots and gates:
                    gate(before(q), v - 1)
                if preps:
                    p = after(q)
                    if v - 2 in SLOT and SLOT[v - 2][0] in ("conv", "z"):
                        silu(p, v - 2)
                    if v == 30:
                        wait(dve, soft_done, count(p, 2, 2))
                        nc.vector.tensor_tensor(delta[:, p[1]], sp_e[:], sp_r[:], ALU.add).then_inc(delta_done, 1)
                    if v == 31:
                        wait(dve, delta_done, count(p, 1, 1))
                        nc.vector.tensor_tensor(du[:, p[1]], delta[:, p[1]], xc[:], ALU.mult).then_inc(du_done, 1)

            def prologue():
                for v in range(32):
                    side_work((-1, 1), v, False, True)
            prologue()

            def add_state(q, n, j):
                wait(dve, hT_done, count(q, 4 * NS, 4 * n + j + 1))
                if n == 0:
                    wait(dve, prep_taken, count(q, PREPS, prep_done("skip", j)))
                else:
                    wait(dve, sum_done, count(q, 4 * NS, 4 * n + j - 3))
                nc.vector.scalar_tensor_tensor(out=acc[:, q[1], j], in0=hT[:, j % 2], scalar=cT[:, q[1], j, n:n + 1],
                                               in1=acc[:, q[1], j], op0=ALU.mult, op1=ALU.add).then_inc(sum_done, 1)

            def scan_block(q, last):
                r = q[1]
                for n in range(NS):
                    for c in range(CH):
                        wait(dve, decay_done, count(q, 4 * NS, 4 * n + c + 1))
                        if c == 0:
                            wait(dve, dbu_done, count(q, NS, n + 1))
                            wait(dve, hT_done, count(q, 4 * NS, 4 * (n - 1)))
                            if r:
                                wait(dve, end_saved, q[0] * NS + (n + 1))
                        nc.vector.tensor_tensor_scan(h[:, n % 2, c], decay[:, c % 2], dbu[:, n % 2, c],
                                                     h_end[:, n, c:c + 1] if r else 0.0,
                                                     ALU.mult, ALU.add).then_inc(scan_done, 1)
                        if n:
                            add_state(q, n - 1, c)
                        elif not first(q):
                            add_state(before(q), NS - 1, c)
                        if c % 2:
                            side_work(q, 2 * n + c // 2, not first(q), not last)
                    if not r:
                        wait(dve, scan_done, count(q, 4 * NS, 4 * (n + 1)))
                        nc.vector.tensor_copy(h_end[:, n], h[:, n % 2, :, T - 1]).then_inc(end_saved, 1)

            def body(b, last):
                for half in range(HALVES):
                    scan_block((b, half), last and half == HALVES - 1)
            sequences(dve, body)
            q = (S - 1, HALVES - 1)
            for j in range(TB):
                add_state(q, NS - 1, j)
            for v in gate_slots:
                gate(q, v)

        @block.tensor
        def _(pe):
            pe.wait_ge(s_diag, 1)
            pe.wait_ge(s_const, 7)
            pe.wait_ge(s_weights, 16 * 8)

            def bank_free(q, v, preps):
                if v < 4 and q[0] is S:
                    return
                if v < 4:
                    wait(pe, prep_taken, count(q, PREPS, PREPS - 3 + v))
                elif SLOT[v - 2][0] in VECTOR_KINDS:
                    wait(pe, gate_taken, count(before(q), GATES, 1 + gate_slots.index(v - 2)))
                elif preps:
                    wait(pe, prep_taken, count(after(q), PREPS, prep_done(*SLOT[v - 2])))

            def slot(q, v, gates, preps, tail=False):
                if v not in SLOT:
                    return
                kind, i = SLOT[v]
                if not (gates if kind in VECTOR_KINDS else preps):
                    return
                bank = slot_bank[:, v % 2]
                if not tail:
                    bank_free(q, v, preps)
                if kind in VECTOR_KINDS:
                    g = before(q)
                    if kind == "y":
                        if i == 0:
                            wait(pe, sum_done, count(g, 4 * NS, 4 * NS))
                        for j in range(TB):
                            ins = nc.tensor.transpose(bank[:, j * P:(j + 1) * P],
                                                      acc[:, g[1], j, i * P:(i + 1) * P], ident[:])
                    else:
                        wait(pe, gate_taken, count(g, GATES, CH))
                        for j in range(2):
                            t = (2 * i + j) * P
                            for c in range(CH):
                                ins = nc.tensor.matmul(bank[:, j * H:(j + 1) * H], y[:, c, t:t + P], w_out[:, c],
                                                       start=(c == 0), stop=(c == CH - 1))
                    ins.then_inc(gate_made, 1)
                    return
                p = after(q)
                if kind == "xnT":
                    if i == 0:
                        wait(pe, ln_done, count(p, 1, 1))
                        wait(pe, prep_taken, count(q, PREPS, PREPS))
                    for j in range(TB):
                        ins = nc.tensor.transpose(bank[:, j * P:(j + 1) * P], xn[:, j, i * P:(i + 1) * P], ident[:])
                elif kind in ("x", "z"):
                    col = i * P + (DI if kind == "z" else 0)
                    wait(pe, prep_taken, count(p, PREPS, prep_done("xnT", KH - 1)))
                    for k in range(KH):
                        ins = nc.tensor.matmul(bank, w_in[:, k, col:col + P], xnT[:, k],
                                               start=(k == 0), stop=(k == KH - 1))
                elif kind == "conv":
                    wait(pe, prep_taken, count(p, PREPS, prep_done("x", i)))
                    for k in range(TAPS):
                        ins = nc.tensor.matmul(bank, tap_diag[:, i, k], xpad[:, i, k:k + T],
                                               start=(k == 0), stop=(k == TAPS - 1))
                elif kind == "dbl":
                    wait(pe, silu_done, count(p, 2 * CH, CH))
                    for c in range(CH):
                        ins = nc.tensor.matmul(bank, w_x[:, c], xc[:, c], start=(c == 0), stop=(c == CH - 1))
                elif kind == "dt":
                    wait(pe, prep_taken, count(p, PREPS, prep_done("dbl", 0)))
                    ins = nc.tensor.matmul(bank, w_dt[:, i * P:(i + 1) * P], dbl[0:R, p[1]], start=True, stop=True)
                elif kind == "C":
                    for j in range(TB):
                        ins = nc.tensor.transpose(bank[:, j * P:(j + 1) * P], dbl[:, p[1], j * P:(j + 1) * P], ident[:])
                elif kind == "skip":
                    for c in range(CH):
                        ins = nc.tensor.matmul(bank[:, c * P:(c + 1) * P], xc[:, c, i * P:(i + 1) * P],
                                               skip_diag[:, c], start=True, stop=True)
                ins.then_inc(prep_made, 1)

            for v in range(32):
                slot((-1, 1), v, False, True)

            def spread_b(q, n):
                wait(pe, bb_done, count(q, NS, n - 1))
                if n == 0:
                    wait(pe, prep_taken, count(q, PREPS, prep_done("dbl", 0)))
                nc.tensor.matmul(bcast[:, n % 2], pick[R:R + NS, n], dbl[R:R + NS, q[1]],
                                 start=True, stop=True).then_inc(bcast_made, 1)

            def turn(q, n, j):
                if j == 0:
                    wait(pe, scan_done, count(q, 4 * NS, 4 * (n + 1)))
                wait(pe, sum_done, count(q, 4 * NS, 4 * n + j - 1))
                for c in range(CH):
                    ins = nc.tensor.transpose(hT[:, j % 2, c * P:(c + 1) * P], h[:, n % 2, c, j * P:(j + 1) * P],
                                              ident[:])
                ins.then_inc(hT_done, 1)

            def scan_block(q, last):
                gates, preps = not first(q), not last
                spread_b(q, 0)
                for n in range(NS):
                    if n < NS - 1:
                        spread_b(q, n + 1)
                    for half in range(2):
                        for j in (2 * half, 2 * half + 1):
                            if n:
                                turn(q, n - 1, j)
                            elif not first(q):
                                turn(before(q), NS - 1, j)
                        slot(q, 2 * n + half, gates, preps)

            def body(b, last):
                for half in range(HALVES):
                    scan_block((b, half), last and half == HALVES - 1)
            sequences(pe, body)
            q = (S - 1, HALVES - 1)
            for j in range(TB):
                turn(q, NS - 1, j)
            wait(pe, gate_taken, count(before(q), GATES, GATES))
            for v in gate_slots:
                if v - 2 in gate_slots[:CH]:
                    wait(pe, gate_taken, count(q, GATES, 1 + gate_slots.index(v - 2)))
                slot((S, 0), v, True, False, tail=True)


def attention_stage(nc, x1, w, base, n2, logits, slot_rows, slot_out):
    PLACES = P
    BLOCKS = L // PLACES
    GL = 16
    GROUPS = PLACES // GL
    PAIR = HEADS // KV
    NORM_T, QKV, PROJ, NORM2_T = 8, 16, 8, 8
    ACT_TAKES = NORM_T + QKV + NORM2_T

    with ExitStack() as ctx:
        al = Allocator(nc, ctx, "a_")
        sb, sem = al.sb, al.sem
        w_qkv = sb("w_qkv", [P, KH, 4 * P])
        w_proj = sb("w_proj", [P, PAIR, H])
        w_router = sb("w_router", [P, KH, EXPERTS])
        ln_vecs = sb("ln_vecs", [P, 4, KH])
        ident = sb("ident", [P, P])
        head_mask = sb("head_mask", [P, KV])
        causal = sb("causal", [P, NS])
        s_of_p = sb("s_of_p", [P, NS])
        row_i = sb("row_i", [P, NS], I32)
        col_i = sb("col_i", [P, NS], I32)
        minus_half = sb("minus_half", [P, S])
        eps = sb("eps", [P, S])
        xa = sb("xa", [P, S, H])
        zeros = sb("zeros", [P, 2048])
        u = sb("u", [P, S, H])
        stats = sb("stats", [P, S, 6])
        moments = sb("moments", [P, S, 2])
        rstd = sb("rstd", [P, S])
        n1 = sb("n1", [P, S, H])
        oT = n1[:].rearrange("p (a s) m -> p a (s m)", a=PAIR).rearrange("p a (s l) -> p a s l", s=S)
        xT = sb("xT", [P, KH, S, P])
        qT = sb("qT", [P, PAIR, S, P])
        kT = sb("kT", [P, S, P])
        vT = sb("vT", [P, S, P])
        kx = sb("kx", [P, 2, GL, KV, S])
        vx = sb("vx", [P, 2, GL, KV, S])
        vbd = sb("vbd", [P, 2, GL, P])
        sm = sb("sm", [P, 2, 4 * KV, S])
        mx = sb("mx", [P, 2, 4 * KV])
        pT = sb("pT", [P, 2, 4 * P])
        lg = sb("lg", [P, S, EXPERTS])
        common = al.ps("common", [P, 2, 512])
        score = al.ps("score", [P, 2, 512])
        vbank = al.ps("vbank", [P, 2, 512])
        pbank = al.ps("pbank", [P, 512])
        obank = al.ps("obank", [P, 512])

        s_w = sem("weights")
        s_const = sem("const")
        zeroed, cleared = sem("zeroed"), sem("cleared")
        mask_step = sem("mask_step")
        x_loaded = sem("x_loaded")
        base_stored = sem("base_stored")
        n2_stored = sem("n2_stored")
        lg_stored = sem("lg_stored")
        moments_done = sem("moments_done")
        rstd_done = sem("rstd_done")
        u_done = sem("u_done")
        n1_done = sem("n1_done")
        made = sem("made")
        act_took = sem("act_took")
        dve_took = sem("dve_took")
        kx_done = sem("kx_done")
        vx_done = sem("vx_done")
        score_made = sem("score_made")
        vbank_made = sem("vbank_made")
        vbd_done = sem("vbd_done")
        soft = sem("soft")
        exp_done = sem("exp_done")
        pbank_made = sem("pbank_made")
        pbank_took = sem("pbank_took")
        obank_made = sem("obank_made")
        o_done = sem("o_done")
        base_done = sem("base_done")
        n2_done = sem("n2_done")
        dve_passed, sp_passed = sem("dve_passed"), sem("sp_passed")

        x1_b = x1.rearrange("s (b p) m -> b p s m", p=P)
        base_b = base.rearrange("s (b p) m -> b p s m", p=P)
        n2_b = n2.rearrange("s (b p) m -> b p s m", p=P)

        block = ctx.enter_context(nc.Block())

        def at(b, per_block, done):
            return b * per_block + done

        def blocks(eng, body):
            body(0)
            with eng.Fori(1, BLOCKS) as b:
                body(b)

        @block.sync
        def _(sp):
            for dst, src in ((w_qkv[:], w["qkv_T"].rearrange("(k p) e -> p k e", p=P)),
                             (w_proj[:], w["proj_T"].rearrange("(a p) m -> p a m", p=P)),
                             (w_router[:], w["router"].rearrange("(k p) e -> p k e", p=P)),
                             (ln_vecs[:], w["ln_vecs"])):
                sp.dma_start(dst, src).then_inc(s_w, 16)

            def clear():
                sp.wait_ge(zeroed, 1)
                for dst in (slot_rows, slot_out[SLOTS:SLOTS + P, :]):
                    flat = dst.rearrange("(p r) m -> p (r m)", p=P)
                    size = flat.shape[1]
                    n = size // 2048
                    if n:
                        sp.dma_start(flat[:, 0:n * 2048].rearrange("p (n c) -> p n c", n=n),
                                     zeros[:].unsqueeze(1).to_broadcast([P, n, 2048])).then_inc(cleared, 16)
                    if size - n * 2048:
                        sp.dma_start(flat[:, n * 2048:], zeros[:, 0:size - n * 2048]).then_inc(cleared, 16)

            def body(b):
                wait_apart(sp, base_stored, at(b, 16, 0), sp_passed)
                sp.dma_start(xa[:], x1_b[b]).then_inc(x_loaded, 16)
                if isinstance(b, int):
                    clear()
                wait_apart(sp, base_done, at(b, 1, 1), sp_passed)
                sp.dma_start(base_b[b], xa[:]).then_inc(base_stored, 16)
                wait_apart(sp, n2_done, at(b, 1, 1), sp_passed)
                sp.dma_start(n2_b[b], n1[:]).then_inc(n2_stored, 16)
                wait_apart(sp, pbank_took, at(b, GROUPS + 1, GROUPS + 1), sp_passed)
                sp.dma_start(logits[b], lg[:]).then_inc(lg_stored, 16)
            blocks(sp, body)
            for done in (base_stored, n2_stored, lg_stored):
                sp.wait_ge(done, 16 * BLOCKS)
            sp.wait_ge(cleared, 16 * 3)

        @block.gpsimd
        def _(pool):
            nc.gpsimd.memset(zeros[:], 0.0).then_inc(zeroed, 1)
            nc.gpsimd.memset(minus_half[:], -0.5).then_inc(s_const, 1)
            nc.gpsimd.memset(eps[:], EPS).then_inc(s_const, 1)
            nc.gpsimd.memset(ident[:], 0.0).then_inc(s_const, 1)
            nc.gpsimd.memset(head_mask[:], 1.0).then_inc(s_const, 1)
            nc.gpsimd.iota(row_i[:], pattern=[[0, NS]], base=0, channel_multiplier=1).then_inc(s_const, 1)
            nc.gpsimd.iota(col_i[:], pattern=[[1, NS]], base=0, channel_multiplier=0).then_inc(s_const, 1)
            pool.wait_ge(s_const, 6)
            nc.gpsimd.affine_select(out=ident[:], in_=ident[:], compare_op=ALU.not_equal, fill=1.0,
                                    base=0, pattern=[[-1, P]], channel_multiplier=1).then_inc(s_const, 1)
            nc.gpsimd.affine_select(out=head_mask[:], in_=head_mask[:], compare_op=ALU.is_ge, fill=0.0,
                                    base=0, pattern=[[-HD, KV]], channel_multiplier=1).then_inc(s_const, 1)
            pool.wait_ge(s_const, 8)
            nc.gpsimd.affine_select(out=head_mask[:], in_=head_mask[:], compare_op=ALU.is_ge, fill=0.0,
                                    base=HD - 1, pattern=[[HD, KV]], channel_multiplier=-1).then_inc(s_const, 1)

            def inverse_deviation(b, k):
                wait(pool, moments_done, at(b, 6, 2 * k + 2))
                nc.gpsimd.tensor_tensor(rstd[:], moments[:, :, 1], eps[:], ALU.add).then_inc(rstd_done, 1)
                wait(pool, rstd_done, at(b, 6, 2 * k + 1))
                nc.gpsimd.tensor_tensor(rstd[:], rstd[:], minus_half[:], ALU.pow).then_inc(rstd_done, 1)

            def body(b):
                inverse_deviation(b, 0)
                inverse_deviation(b, 1)
                wait(pool, act_took, at(b, ACT_TAKES, NORM_T + QKV))
                for i in range(GROUPS):
                    wait(pool, score_made, at(b, GROUPS, i - 1))
                    nc.gpsimd.tensor_tensor(
                        kx[:, i % 2],
                        kT[:, :, i * GL:(i + 1) * GL].rearrange("p s l -> p l s").unsqueeze(2).to_broadcast([P, GL, KV, S]),
                        head_mask[:].unsqueeze(1).unsqueeze(3).to_broadcast([P, GL, KV, S]),
                        ALU.mult).then_inc(kx_done, 1)
                wait(pool, dve_took, at(b, PROJ, PROJ))
                nc.gpsimd.tensor_tensor(xa[:], xa[:], u[:], ALU.add).then_inc(base_done, 1)
                inverse_deviation(b, 2)
            blocks(pool, body)

        @block.scalar
        def _(act):
            act.wait_ge(s_w, 16 * 4)

            def body(b):
                def take_norm(k4, first_use, row):
                    k, t4 = k4 // 4, k4 % 4
                    wait(act, made, at(b, NORM_T + QKV + PROJ + NORM2_T, first_use + k4 + 1))
                    nc.scalar.activation(xT[:, k, 4 * t4:4 * t4 + 4].rearrange("p s l -> p (s l)"),
                                         common[:, k4 % 2], ACT.Identity,
                                         scale=ln_vecs[:, row, k:k + 1], bias=ln_vecs[:, row + 1, k:k + 1]).then_inc(act_took, 1)
                wait(act, pbank_made, at(b, GROUPS + 1, 0))
                for k4 in range(NORM_T):
                    take_norm(k4, 0, 0)
                for m in range(4):
                    for t4 in range(4):
                        n = 4 * m + t4
                        wait(act, made, at(b, NORM_T + QKV + PROJ + NORM2_T, NORM_T + n + 1))
                        dst = (qT[:, 0], qT[:, 1], kT[:], vT[:])[m][:, 4 * t4:4 * t4 + 4].rearrange("p s l -> p (s l)")
                        nc.scalar.activation(dst, common[:, n % 2], ACT.Copy,
                                             scale=HD ** -0.5 if m < 2 else 1.0).then_inc(act_took, 1)
                def take_values(i):
                    for k in range(4):
                        wait(act, vbank_made, at(b, 4 * GROUPS, 4 * i + k + 1))
                        if k == 0:
                            wait(act, obank_made, at(b, GROUPS, i - 1))
                        nc.scalar.copy(vbd[:, i % 2, 4 * k:4 * k + 4].rearrange("p l d -> p (l d)"),
                                       vbank[:, k % 2]).then_inc(vbd_done, 1)
                def take_probs(i):
                    wait(act, pbank_made, at(b, GROUPS + 1, i + 1))
                    wait(act, obank_made, at(b, GROUPS, i - 1))
                    nc.scalar.copy(pT[:, i % 2], pbank[:]).then_inc(pbank_took, 1)
                for i in range(GROUPS):
                    take_values(i)
                    wait(act, soft, at(b, 6 * GROUPS, 6 * i + 3))
                    nc.scalar.activation(sm[:, i % 2], sm[:, i % 2], ACT.Exp).then_inc(exp_done, 1)
                    if i:
                        take_probs(i - 1)
                take_probs(GROUPS - 1)
                for k4 in range(NORM2_T):
                    take_norm(k4, NORM_T + QKV + PROJ, 2)
                wait(act, pbank_made, at(b, GROUPS + 1, GROUPS + 1))
                wait(act, lg_stored, at(b, 16, 0))
                nc.scalar.copy(lg[:].rearrange("p s e -> p (s e)"), pbank[:, 0:S * EXPERTS]).then_inc(pbank_took, 1)
            blocks(act, body)

        @block.vector
        def _(dve):
            dve.wait_ge(s_const, 9)
            nc.vector.tensor_single_scalar(row_i[:], row_i[:], S - 1, op=ALU.bitwise_and).then_inc(mask_step, 1)
            nc.vector.tensor_copy(causal[:], col_i[:]).then_inc(mask_step, 1)
            dve.wait_ge(mask_step, 2)
            nc.vector.tensor_copy(s_of_p[:], row_i[:]).then_inc(mask_step, 1)
            dve.wait_ge(mask_step, 3)
            nc.vector.tensor_tensor(causal[:], causal[:], s_of_p[:], ALU.is_gt).then_inc(mask_step, 1)
            dve.wait_ge(mask_step, 4)
            nc.vector.tensor_scalar(causal[:], causal[:], -1.0e9, None, ALU.mult).then_inc(mask_step, 1)
            dve.wait_ge(mask_step, 5)

            def body(b):
                def moments_of(src, k):
                    for s in range(S):
                        ins = nc.vector.bn_stats(stats[:, s], src[:, s])
                    ins.then_inc(moments_done, 1)
                    wait_apart(dve, moments_done, at(b, 6, 2 * k + 1), dve_passed)
                    for s in range(S):
                        ins = nc.vector.bn_aggr(moments[:, s], stats[:, s])
                    ins.then_inc(moments_done, 1)
                    wait(dve, rstd_done, at(b, 6, 2 * k + 2))

                def normalise(dst, src, done):
                    for s in range(S):
                        ins = nc.vector.tensor_scalar(dst[:, s], src[:, s], moments[:, s, 0:1], rstd[:, s:s + 1],
                                                      ALU.subtract, ALU.mult)
                    ins.then_inc(done, 1)

                wait(dve, x_loaded, at(b, 16, 16))
                moments_of(xa, 0)
                normalise(u, xa, u_done)
                wait(dve, u_done, at(b, 1, 1))
                moments_of(u, 1)
                wait(dve, n2_stored, at(b, 16, 0))
                normalise(n1, u, n1_done)
                wait(dve, act_took, at(b, ACT_TAKES, NORM_T + QKV))

                def spread_values(i):
                    wait(dve, vbank_made, at(b, 4 * GROUPS, 4 * (i - 1)))
                    nc.vector.tensor_tensor(
                        vx[:, i % 2],
                        vT[:, :, i * GL:(i + 1) * GL].rearrange("p s l -> p l s").unsqueeze(2).to_broadcast([P, GL, KV, S]),
                        head_mask[:].unsqueeze(1).unsqueeze(3).to_broadcast([P, GL, KV, S]),
                        ALU.mult).then_inc(vx_done, 1)

                def softmax_before(i):
                    x = sm[:, i % 2]
                    wait(dve, score_made, at(b, GROUPS, i + 1))
                    wait(dve, pbank_made, at(b, GROUPS + 1, i - 1))
                    nc.vector.tensor_tensor(x, score[:, i % 2].rearrange("p (g t) -> p g t", t=S),
                                            causal[:].unsqueeze(1).to_broadcast([P, 4 * KV, S]), ALU.add).then_inc(soft, 1)
                    wait(dve, soft, at(b, 6 * GROUPS, 6 * i + 1))
                    nc.vector.reduce_max(mx[:, i % 2], x, axis=AXX).then_inc(soft, 1)
                    wait(dve, soft, at(b, 6 * GROUPS, 6 * i + 2))
                    nc.vector.tensor_tensor(x, x, mx[:, i % 2].unsqueeze(2).to_broadcast([P, 4 * KV, S]),
                                            ALU.subtract).then_inc(soft, 1)

                def softmax_after(i):
                    x = sm[:, i % 2]
                    wait(dve, exp_done, at(b, GROUPS, i + 1))
                    nc.vector.reduce_sum(mx[:, i % 2], x, axis=AXX).then_inc(soft, 1)
                    wait(dve, soft, at(b, 6 * GROUPS, 6 * i + 4))
                    nc.vector.reciprocal(mx[:, i % 2], mx[:, i % 2]).then_inc(soft, 1)
                    wait(dve, soft, at(b, 6 * GROUPS, 6 * i + 5))
                    nc.vector.tensor_tensor(x, x, mx[:, i % 2].unsqueeze(2).to_broadcast([P, 4 * KV, S]),
                                            ALU.mult).then_inc(soft, 1)

                def take_output(i):
                    wait(dve, obank_made, at(b, GROUPS, i + 1))
                    if i == 0:
                        wait(dve, made, at(b, NORM_T + QKV + PROJ + NORM2_T, NORM_T))
                    nc.vector.tensor_copy(
                        oT[:, :, :, i * GL:(i + 1) * GL].rearrange("p a s l -> p l (a s)"),
                        obank[:].rearrange("p (l r) -> p l r", l=GL)).then_inc(o_done, 1)

                spread_values(0)
                for i in range(GROUPS):
                    if i < GROUPS - 1:
                        spread_values(i + 1)
                    softmax_before(i)
                    if i >= 2:
                        take_output(i - 2)
                    softmax_after(i)
                take_output(GROUPS - 2)
                take_output(GROUPS - 1)
                for i in range(PROJ):
                    wait(dve, made, at(b, NORM_T + QKV + PROJ + NORM2_T, NORM_T + QKV + i + 1))
                    nc.vector.tensor_tensor(u[:, 2 * i:2 * i + 2], common[:, i % 2].rearrange("p (j m) -> p j m", j=2),
                                            u[:, 2 * i:2 * i + 2], ALU.add).then_inc(dve_took, 1)
                wait(dve, dve_took, at(b, PROJ, PROJ))
                moments_of(u, 2)
                normalise(n1, u, n2_done)
            blocks(dve, body)

        @block.tensor
        def _(pe):
            pe.wait_ge(s_w, 16 * 4)
            pe.wait_ge(s_const, 9)
            USES = NORM_T + QKV + PROJ + NORM2_T

            def body(b):
                def common_free(use):
                    prev = use - 2
                    if prev < 0:
                        wait(pe, act_took, at(b, ACT_TAKES, prev + 1))
                    elif prev < NORM_T + QKV:
                        wait(pe, act_took, at(b, ACT_TAKES, prev + 1))
                    elif prev < NORM_T + QKV + PROJ:
                        wait(pe, dve_took, at(b, PROJ, prev - (NORM_T + QKV) + 1))
                    else:
                        wait(pe, act_took, at(b, ACT_TAKES, prev - PROJ + 1))

                def turn_norm(first_use):
                    for k4 in range(8):
                        common_free(first_use + k4)
                        k, t4 = k4 // 4, k4 % 4
                        for s in range(4):
                            ins = nc.tensor.transpose(common[:, k4 % 2, s * P:(s + 1) * P],
                                                      n1[:, 4 * t4 + s, k * P:(k + 1) * P], ident[:])
                        ins.then_inc(made, 1)

                wait(pe, n1_done, at(b, 1, 1))
                turn_norm(0)
                for m in range(4):
                    for t4 in range(4):
                        use = NORM_T + 4 * m + t4
                        common_free(use)
                        wait(pe, act_took, at(b, ACT_TAKES, NORM_T))
                        for k in range(KH):
                            ins = nc.tensor.matmul(common[:, use % 2], w_qkv[:, k, m * P:(m + 1) * P],
                                                   xT[:, k, 4 * t4:4 * t4 + 4].rearrange("p s l -> p (s l)"),
                                                   start=(k == 0), stop=(k == KH - 1))
                        ins.then_inc(made, 1)

                def scores(i):
                    wait(pe, act_took, at(b, ACT_TAKES, NORM_T + QKV))
                    wait(pe, kx_done, at(b, GROUPS, i + 1))
                    wait(pe, soft, at(b, 6 * GROUPS, 6 * (i - 2) + 1))
                    for l in range(GL):
                        r, col = 32 * (l % 4), P * (l // 4)
                        ins = nc.tensor.matmul(score[r:r + 32, i % 2, col:col + P],
                                               qT[:, :, :, i * GL + l].rearrange("p a s -> p (a s)"),
                                               kx[:, i % 2, l].rearrange("p g t -> p (g t)"), start=True, stop=True)
                    ins.then_inc(score_made, 1)

                def turn_values(i):
                    wait(pe, vx_done, at(b, GROUPS, i + 1))
                    for k in range(4):
                        wait(pe, vbd_done, at(b, 4 * GROUPS, 4 * i + k - 1))
                        for l in range(4):
                            ins = nc.tensor.transpose(vbank[:, k % 2, l * P:(l + 1) * P],
                                                      vx[:, i % 2, 4 * k + l].rearrange("p g t -> p (g t)"), ident[:])
                        ins.then_inc(vbank_made, 1)

                def turn_probs(i):
                    wait(pe, soft, at(b, 6 * GROUPS, 6 * i + 6))
                    wait(pe, pbank_took, at(b, GROUPS + 1, i))
                    for k in range(4):
                        ins = nc.tensor.transpose(pbank[:, k * P:(k + 1) * P],
                                                  sm[:, i % 2, k * KV:(k + 1) * KV].rearrange("p g t -> p (g t)"), ident[:])
                    ins.then_inc(pbank_made, 1)

                def outputs(i):
                    wait(pe, pbank_took, at(b, GROUPS + 1, i + 1))
                    wait(pe, vbd_done, at(b, 4 * GROUPS, 4 * i + 4))
                    wait(pe, o_done, at(b, GROUPS, i))
                    for l in range(GL):
                        ins = nc.tensor.matmul(obank[:, 32 * l:32 * l + 32], vbd[:, i % 2, l],
                                               pT[:, i % 2, 32 * l:32 * l + 32], start=True, stop=True)
                    ins.then_inc(obank_made, 1)

                for i in range(GROUPS):
                    scores(i)
                    turn_values(i)
                    if i:
                        turn_probs(i - 1)
                        outputs(i - 1)
                turn_probs(GROUPS - 1)
                outputs(GROUPS - 1)
                wait(pe, o_done, at(b, GROUPS, GROUPS))
                for i in range(PROJ):
                    common_free(NORM_T + QKV + i)
                    for j in range(2):
                        for a in range(PAIR):
                            ins = nc.tensor.matmul(common[:, i % 2, j * H:(j + 1) * H], oT[:, a, 2 * i + j],
                                                   w_proj[:, a], start=(a == 0), stop=(a == PAIR - 1))
                    ins.then_inc(made, 1)
                wait(pe, n2_done, at(b, 1, 1))
                turn_norm(NORM_T + QKV + PROJ)
                wait(pe, act_took, at(b, ACT_TAKES, ACT_TAKES))
                wait(pe, pbank_took, at(b, GROUPS + 1, GROUPS))
                for s in range(S):
                    for k in range(KH):
                        ins = nc.tensor.matmul(pbank[:, s * EXPERTS:(s + 1) * EXPERTS], xT[:, k, s], w_router[:, k],
                                               start=(k == 0), stop=(k == KH - 1))
                ins.then_inc(pbank_made, 1)
            blocks(pe, body)


def routing_stage(nc, logits, slot_of, weight_of):
    TILES = TOKENS // P
    B = L // P
    E = EXPERTS
    with ExitStack() as ctx:
        al = Allocator(nc, ctx, "r_")
        sb, sem = al.sb, al.sem
        raw = sb("raw", [P, B, S, E])
        prob = sb("prob", [P, TILES, E])
        best = [sb("best0", [P, TILES, E]), sb("best1", [P, TILES, E])]
        work = sb("work", [P, TILES, E])
        rank = sb("rank", [P, TILES, E])
        chosen = sb("chosen", [P, TILES, E])
        top = sb("top", [P, TOPK, TILES])
        line = sb("line", [P, TILES])
        kept = sb("kept", [P, TOPK, TILES])
        slot_f = sb("slot_f", [P, TOPK, TILES])
        desc = sb("desc", [P, E])
        first_slot = sb("first_slot", [P, E])
        ones = sb("ones", [P, P])
        earlier = sb("earlier", [P, P])
        within = al.ps("within", [P, TILES, E])
        total = al.ps("total", [P, TILES, E])
        loaded = sem("loaded")
        const = sem("const")
        step = sem("step")
        exped = sem("exped")
        counted = sem("counted")
        CONST = 3 + 2 * E
        STEP_CHOSEN = 19
        block = ctx.enter_context(nc.Block())

        @block.sync
        def _(sp):
            sp.dma_start(raw[:], logits.rearrange("b p s e -> p b s e")).then_inc(loaded, 16)

        @block.gpsimd
        def _(pool):
            nc.gpsimd.memset(ones[:], 1.0).then_inc(const, 1)
            nc.gpsimd.memset(earlier[:], 1.0).then_inc(const, 1)
            for e in range(E):
                nc.gpsimd.memset(desc[:, e:e + 1], float(E - e)).then_inc(const, 1)
                nc.gpsimd.memset(first_slot[:, e:e + 1], float(e * CAP)).then_inc(const, 1)
            pool.wait_ge(const, 2)
            nc.gpsimd.affine_select(out=earlier[:], in_=earlier[:], compare_op=ALU.is_gt, fill=0.0,
                                    base=0, pattern=[[1, P]], channel_multiplier=-1).then_inc(const, 1)
        @block.scalar
        def _(act):
            act.wait_ge(step, 3)
            nc.scalar.activation(prob[:], prob[:], ACT.Exp).then_inc(exped, 1)

        @block.tensor
        def _(pe):
            pe.wait_ge(const, CONST)
            pe.wait_ge(step, STEP_CHOSEN)
            for half in range(2):
                part = slice(half * TILES // 2, (half + 1) * TILES // 2)
                nc.tensor.matmul(within[:, part].rearrange("p t e -> p (t e)"), earlier[:],
                                 chosen[:, part].rearrange("p t e -> p (t e)"), start=True, stop=True)
                ins = nc.tensor.matmul(total[:, part].rearrange("p t e -> p (t e)"), ones[:],
                                       chosen[:, part].rearrange("p t e -> p (t e)"), start=True, stop=True)
            ins.then_inc(counted, 1)

        @block.vector
        def _(dve):
            n = [0]

            def after_last(ins):
                n[0] += 1
                ins.then_inc(step, 1)
                dve.wait_ge(step, n[0])

            def per_token(x):
                return x.unsqueeze(2).to_broadcast([P, TILES, E])

            def per_expert(x):
                return x.unsqueeze(1).to_broadcast([P, TILES, E])

            tt = nc.vector.tensor_tensor
            dve.wait_ge(const, CONST)
            dve.wait_ge(loaded, 16)
            after_last(nc.vector.tensor_copy(prob[:].rearrange("p (s b) e -> p b s e", b=B), raw[:]))
            after_last(nc.vector.reduce_max(line[:], prob[:], axis=AXX))
            after_last(tt(prob[:], prob[:], per_token(line[:]), ALU.subtract))
            dve.wait_ge(exped, 1)
            after_last(nc.vector.reduce_sum(line[:], prob[:], axis=AXX))
            after_last(nc.vector.reciprocal(line[:], line[:]))
            after_last(tt(prob[:], prob[:], per_token(line[:]), ALU.mult))
            for k in range(TOPK):
                after_last(nc.vector.reduce_max(top[:, k], prob[:], axis=AXX))
                after_last(tt(work[:], prob[:], per_token(top[:, k]), ALU.is_equal))
                after_last(tt(work[:], work[:], per_expert(desc[:]), ALU.mult))
                after_last(nc.vector.reduce_max(line[:], work[:], axis=AXX))
                after_last(tt(best[k][:], per_token(line[:]), per_expert(desc[:]), ALU.is_equal))
                if k == 0:
                    after_last(nc.vector.scalar_tensor_tensor(out=prob[:], in0=best[0][:], scalar=-2.0, in1=prob[:],
                                                              op0=ALU.mult, op1=ALU.add))
            after_last(tt(chosen[:], best[0][:], best[1][:], ALU.add))
            after_last(tt(line[:], top[:, 0], top[:, 1], ALU.add))
            assert n[0] == STEP_CHOSEN, n
            after_last(nc.vector.reciprocal(line[:], line[:]))
            for k in range(TOPK):
                after_last(tt(top[:, k], top[:, k], line[:], ALU.mult))
            dve.wait_ge(counted, 1)
            for e in range(E):
                ins = nc.vector.tensor_tensor_scan(rank[:, :, e], ones[:, 0:TILES], total[:, :, e], 0.0,
                                                   ALU.mult, ALU.add)
            after_last(ins)
            after_last(tt(rank[:], rank[:], total[:], ALU.subtract))
            after_last(tt(rank[:], rank[:], within[:], ALU.add))
            after_last(nc.vector.tensor_scalar(work[:], rank[:], float(CAP), None, ALU.is_lt))
            after_last(tt(rank[:], rank[:], per_expert(first_slot[:]), ALU.add))
            for k in range(TOPK):
                after_last(tt(prob[:], best[k][:], work[:], ALU.mult))
                after_last(nc.vector.reduce_sum(kept[:, k], prob[:], axis=AXX))
                after_last(tt(prob[:], best[k][:], rank[:], ALU.mult))
                after_last(nc.vector.reduce_sum(slot_f[:, k], prob[:], axis=AXX))
            after_last(tt(weight_of[:], top[:], kept[:], ALU.mult))
            after_last(nc.vector.scalar_tensor_tensor(out=slot_f[:], in0=slot_f[:], scalar=float(-SLOTS), in1=kept[:],
                                                      op0=ALU.add, op1=ALU.mult))
            after_last(nc.vector.tensor_scalar(slot_f[:], slot_f[:], float(SLOTS), None, ALU.add))
            after_last(nc.vector.tensor_copy(slot_of[:], slot_f[:]))


def in_pairs(eng, body):
    body(0)
    with eng.Fori(1, S // 2 - 1) as pair:
        body(pair)
    body(S // 2 - 1)


def dispatch_stage(nc, n2, slot_of, slot_rows):
    B = L // P
    with ExitStack() as ctx:
        al = Allocator(nc, ctx, "d_")
        rows = al.sb("rows", [P, 2, B, H])
        index = al.sb("index", [P, 2, TOPK, B], I32)
        loaded = [al.sem("loaded0"), al.sem("loaded1")]
        scattered = [al.sem("scattered0"), al.sem("scattered1")]
        indexed = al.sem("indexed")
        passed, passed_pool = al.sem("passed"), al.sem("passed_pool")
        PER_S = 16 * TOPK * B
        block = ctx.enter_context(nc.Block())

        @block.sync
        def _(sp):
            def body(pair):
                for half in range(2):
                    wait_apart(sp, scattered[half], pair * PER_S, passed)
                    sp.dma_start(rows[:, half], n2.rearrange("s (b p) m -> s p b m", p=P)[2 * pair + half]).then_inc(loaded[half], 16)
            in_pairs(sp, body)

        @block.vector
        def _(dve):
            def body(pair):
                for half in range(2):
                    wait(dve, scattered[half], pair * PER_S)
                    col = pair * (2 * B) + half * B
                    nc.vector.tensor_copy(index[:, half], slot_of[:, :, bass.ds(col, B)]).then_inc(indexed, 1)
            in_pairs(dve, body)

        @block.gpsimd
        def _(pool):
            def body(pair):
                for half in range(2):
                    wait(pool, loaded[half], pair * 16 + 16)
                    wait_apart(pool, indexed, pair * 2 + (half + 1), passed_pool)
                    for b in range(B):
                        for k in range(TOPK):
                            nc.gpsimd.indirect_dma_start(
                                slot_rows, bass.IndirectOffsetOnAxis(ap=index[:, half, k, b:b + 1], axis=0),
                                rows[:, half, b], None, bounds_check=SLOTS - 1, oob_is_err=False).then_inc(scattered[half], 16)
            in_pairs(pool, body)
            for half in range(2):
                pool.wait_ge(scattered[half], S // 2 * PER_S)


def expert_stage(nc, w, slot_rows, slot_out):
    SB = 512
    BLOCKS = CAP // SB
    FC = FFN // P
    Y_START, T_START = 2 + 2 * BLOCKS, 4
    with ExitStack() as ctx:
        al = Allocator(nc, ctx, "e_")
        sb, sem = al.sb, al.sem
        w1 = sb("w1", [P, 2, KH, FFN])
        w2 = sb("w2", [P, 2, FC, H])
        ln2 = sb("ln2", [P, 4, KH])
        ident = sb("ident", [P, P])
        xe = sb("xe", [P, 2, 4, H])
        xT = sb("xT", [P, 2, KH, SB])
        a = sb("a", [P, 2, FC, SB])
        ye = sb("ye", [P, 2, 4, H])
        tbank = al.ps("tbank", [P, 2, SB])
        ubank = al.ps("ubank", [P, 2, SB])
        ybank = al.ps("ybank", [P, 2, 4, H])
        ln_loaded = sem("ln_loaded")
        w_loaded = [sem("w_loaded0"), sem("w_loaded1")]
        x_loaded = [sem("x_loaded0"), sem("x_loaded1")]
        const = sem("const")
        t_made, t_free = sem("t_made"), sem("t_free")
        u_made, u_taken = sem("u_made"), sem("u_taken")
        y_made, y_free = sem("y_made"), sem("y_free")
        y_stored, ye_free = sem("y_stored"), sem("ye_free")
        sp_passed = sem("sp_passed")
        pool_passed, pe_passed = sem("pool_passed"), sem("pe_passed")
        x_b = slot_rows.rearrange("(n j p) m -> n p j m", j=4, p=P)
        y_b = slot_out[0:SLOTS, :].rearrange("(n j p) m -> n p j m", j=4, p=P)
        w1_e = w["w1"].rearrange("e (k p) f -> e p k f", p=P)
        w2_e = w["w2"].rearrange("e (c p) m -> e p c m", p=P)
        block = ctx.enter_context(nc.Block())

        def each_block(eng, body, expert=None):
            with eng.Fori(0, EXPERTS // 2) as pair:
                for half in range(2):
                    if expert:
                        expert(pair, half)
                    with eng.Fori(0, BLOCKS // 2) as two:
                        for sub in range(2):
                            body(pair * BLOCKS + two + half * (BLOCKS // 2), half, sub)

        @block.sync
        def _(sp):
            sp.dma_start(ln2[:], w["ln_vecs"]).then_inc(ln_loaded, 16)
            sp.dma_start(xe[:, 0], x_b[0]).then_inc(x_loaded[0], 16)

            def weights(pair, half):
                e = pair * 2 + half
                wait_apart(sp, y_free, e * BLOCKS + (Y_START - BLOCKS), sp_passed)
                sp.dma_start(w1[:, half], w1_e[e]).then_inc(w_loaded[half], 16)
                sp.dma_start(w2[:, half], w2_e[e]).then_inc(w_loaded[half], 16)

            def body(m, half, sub):
                n = m * 2 + sub
                wait_apart(sp, t_free, n * 2 + T_START, sp_passed)
                sp.dma_start(xe[:, 1 - sub], x_b[n + 1]).then_inc(x_loaded[1 - sub], 16)
            each_block(sp, body, weights)

        @block.gpsimd
        def _(pool):
            nc.gpsimd.memset(ident[:], 0.0).then_inc(const, 1)
            pool.wait_ge(const, 1)
            nc.gpsimd.affine_select(out=ident[:], in_=ident[:], compare_op=ALU.not_equal, fill=1.0,
                                    base=0, pattern=[[-1, P]], channel_multiplier=1).then_inc(const, 1)
            pool.sem_inc(ye_free, 2)

            def body(m, half, sub):
                n = m * 2 + sub
                wait_apart(pool, y_free, n + (Y_START + 1), pool_passed)
                nc.gpsimd.dma_start(y_b[n], ye[:, sub]).then_inc(y_stored, 16)
                wait(pool, y_stored, n * 16 + 16)
                pool.sem_inc(ye_free, 1)
            each_block(pool, body)

        @block.scalar
        def _(act):
            act.wait_ge(ln_loaded, 16)
            act.sem_inc(t_free, T_START)
            act.sem_inc(u_taken, 2)

            def take_rows(n, sub):
                for k in range(KH):
                    wait(act, t_made, n * 2 + (k + 1))
                    nc.scalar.activation(xT[:, sub, k], tbank[:, k], ACT.Identity, scale=ln2[:, 2, k:k + 1],
                                         bias=ln2[:, 3, k:k + 1]).then_inc(t_free, 1)

            take_rows(0, 0)

            def body(m, half, sub):
                n = m * 2 + sub
                for c in range(FC):
                    wait(act, u_made, n * FC + (c + 1))
                    nc.scalar.activation(a[:, sub, c], ubank[:, c % 2], ACT.Gelu).then_inc(u_taken, 1)
                take_rows(n + 1, 1 - sub)
            each_block(act, body)

        @block.vector
        def _(dve):
            dve.sem_inc(y_free, Y_START)

            def body(m, half, sub):
                n = m * 2 + sub
                wait(dve, y_made, n + 1)
                wait(dve, ye_free, n + 1)
                nc.vector.tensor_copy(ye[:, sub], ybank[:, sub]).then_inc(y_free, 1)
            each_block(dve, body)

        @block.tensor
        def _(pe):
            pe.wait_ge(const, 2)

            def turn_rows(n, turn, sub):
                wait(pe, x_loaded[sub], turn * 16 + 16)
                for k in range(KH):
                    wait(pe, t_free, n * 2 + (k + T_START - 1))
                    for j in range(4):
                        ins = nc.tensor.transpose(tbank[:, k, j * P:(j + 1) * P], xe[:, sub, j, k * P:(k + 1) * P], ident[:])
                    ins.then_inc(t_made, 1)

            turn_rows(0, 0, 0)

            def weights(pair, half):
                wait_apart(pe, w_loaded[half], pair * 32 + 32, pe_passed)

            def body(m, half, sub):
                n = m * 2 + sub
                wait(pe, t_free, n * 2 + (T_START + 2))
                for c in range(FC):
                    wait(pe, u_taken, n * FC + (c + 1))
                    for k in range(KH):
                        ins = nc.tensor.matmul(ubank[:, c % 2], w1[:, half, k, c * P:(c + 1) * P], xT[:, sub, k],
                                               start=(k == 0), stop=(k == KH - 1))
                    ins.then_inc(u_made, 1)
                turn_rows(n + 1, m + sub, 1 - sub)
                wait(pe, u_taken, n * FC + (FC + 2))
                wait(pe, y_free, n + (Y_START - 1))
                for j in range(4):
                    for c in range(FC):
                        ins = nc.tensor.matmul(ybank[:, sub, j], a[:, sub, c, j * P:(j + 1) * P], w2[:, half, c],
                                               start=(c == 0), stop=(c == FC - 1))
                ins.then_inc(y_made, 1)
            each_block(pe, body, weights)


def combine_stage(nc, base, slot_out, slot_of, weight_of, out):
    B = L // P
    with ExitStack() as ctx:
        al = Allocator(nc, ctx, "c_")
        rows = al.sb("rows", [P, 2, B, H])
        got = al.sb("got", [P, 2, TOPK, B, H])
        index = al.sb("index", [P, 2, TOPK, B], I32)
        weight = al.sb("weight", [P, 2, TOPK, B])
        loaded = [al.sem("loaded0"), al.sem("loaded1")]
        gathered = [al.sem("gathered0"), al.sem("gathered1")]
        stored = [al.sem("stored0"), al.sem("stored1")]
        indexed, first_added, summed = al.sem("indexed"), al.sem("first_added"), al.sem("summed")
        sp_passed, pool_passed, act_passed = al.sem("sp_passed"), al.sem("pool_passed"), al.sem("act_passed")
        PER_S = 16 * TOPK * B
        base_s = base.rearrange("s (b p) m -> s p b m", p=P)
        out_s = out.rearrange("s (b p) m -> s p b m", p=P)
        block = ctx.enter_context(nc.Block())

        @block.sync
        def _(sp):
            def body(pair):
                for half in range(2):
                    wait_apart(sp, stored[half], pair * 16, sp_passed)
                    sp.dma_start(rows[:, half], base_s[2 * pair + half]).then_inc(loaded[half], 16)
            in_pairs(sp, body)

        @block.scalar
        def _(act):
            def body(pair):
                for half in range(2):
                    wait_apart(act, summed, pair * 2 + (half + 1), act_passed)
                    nc.scalar.dma_start(out_s[2 * pair + half], rows[:, half]).then_inc(stored[half], 16)
            in_pairs(act, body)
            for half in range(2):
                act.wait_ge(stored[half], 16 * S // 2)

        @block.gpsimd
        def _(pool):
            def body(pair):
                for half in range(2):
                    wait(pool, summed, pair * 2 + (half - 1))
                    wait_apart(pool, indexed, pair * 4 + 2 * (half + 1), pool_passed)
                    for b in range(B):
                        for k in range(TOPK):
                            nc.gpsimd.indirect_dma_start(
                                got[:, half, k, b], None, slot_out,
                                bass.IndirectOffsetOnAxis(ap=index[:, half, k, b:b + 1], axis=0)).then_inc(gathered[half], 16)
            in_pairs(pool, body)

        @block.vector
        def _(dve):
            def take_index(pair, half):
                wait(dve, gathered[half], pair * PER_S)
                wait(dve, summed, pair * 2 + (half - 1))
                col = pair * (2 * B) + half * B
                nc.vector.tensor_copy(index[:, half], slot_of[:, :, bass.ds(col, B)]).then_inc(indexed, 1)
                nc.vector.tensor_copy(weight[:, half], weight_of[:, :, bass.ds(col, B)]).then_inc(indexed, 1)

            def body(pair):
                for half in range(2):
                    take_index(pair, half)
                for half in range(2):
                    wait(dve, loaded[half], pair * 16 + 16)
                    wait(dve, gathered[half], pair * PER_S + PER_S)
                    wait(dve, indexed, pair * 4 + 2 * (half + 1))
                    for k in range(TOPK):
                        if k:
                            wait(dve, first_added, pair * 2 + (half + 1))
                        for b in range(B):
                            ins = nc.vector.scalar_tensor_tensor(
                                out=rows[:, half, b], in0=got[:, half, k, b], scalar=weight[:, half, k, b:b + 1],
                                in1=rows[:, half, b], op0=ALU.mult, op1=ALU.add)
                        ins.then_inc(summed if k else first_added, 1)
            in_pairs(dve, body)


def build(nc, t, out):
    def scratch(name, shape):
        return nc.dram_tensor(name, shape, F32, kind="Internal").ap()

    x1 = scratch("x1", (S, L, H))
    base = scratch("base", (S, L, H))
    n2 = scratch("n2", (S, L, H))
    logits = scratch("logits", (L // P, P, S, EXPERTS))
    slot_rows = scratch("slot_rows", (SLOTS + 512, H))
    slot_out = scratch("slot_out", (SLOTS + P, H))
    mamba_stage(nc, t["x"], t, x1)
    attention_stage(nc, x1, t, base, n2, logits, slot_rows, slot_out)
    with nc.sbuf_tensor("slot_of", [P, TOPK, TOKENS // P], I32) as slot_of, \
            nc.sbuf_tensor("weight_of", [P, TOPK, TOKENS // P], F32) as weight_of:
        routing_stage(nc, logits, slot_of, weight_of)
        dispatch_stage(nc, n2, slot_of, slot_rows)
        expert_stage(nc, t, slot_rows, slot_out)
        combine_stage(nc, base, slot_out, slot_of, weight_of, out)


def kernel(**inputs):
    import numpy as _np
    import concourse.bacc as _bacc
    from concourse.bass_utils import run_bass_kernel_spmd as _run

    g = {k: _np.asarray(v) for k, v in inputs.items()}
    m, f = "L0_attn_", "L0_ffn_"
    qkv = g[f + "qkv_weight"].reshape(KV, HEADS // KV + 2, HD, H)
    proj = g[f + "proj_weight"].T.reshape(KV, HEADS // KV, HD, H)
    arrays = {
        "x": g[m + "hidden_states"],
        "in_T": g[m + "in_proj_w"].T,
        "x_T": g[m + "x_proj_w"].T,
        "dt_T": g[m + "dt_proj_w"].T,
        "out_T": g[m + "out_proj_w"].T,
        "A_log": g[m + "A_log"],
        "conv_w": g[m + "conv_w"],
        "vecs": _np.stack([g[m + n].reshape(CH, P).T for n in ("conv_b", "dt_proj_b", "D")]),
        "qkv_T": qkv.transpose(1, 0, 2, 3).reshape(4 * P, H).T,
        "proj_T": proj.transpose(1, 0, 2, 3).reshape(2 * P, H),
        "router": g[f + "router_weight"],
        "ln_vecs": _np.stack([g[f + n] for n in ("ln1_weight", "ln1_bias", "ln2_weight", "ln2_bias")]
                             ).reshape(4, KH, P).transpose(2, 0, 1),
        "w1": g[f + "moe_w1"],
        "w2": g[f + "moe_w2"],
    }
    arrays = {k: _np.ascontiguousarray(a) for k, a in arrays.items()}
    nc = _bacc.Bacc("TRN2", target_bir_lowering=False, num_devices=1)
    t = {k: nc.dram_tensor("in_" + k, a.shape, F32, kind="ExternalInput").ap() for k, a in arrays.items()}
    out = nc.dram_tensor("out", (S, L, H), F32, kind="ExternalOutput").ap()
    build(nc, t, out)
    r = _run(nc, [{"in_" + k: a for k, a in arrays.items()}], core_ids=[0])
    return r.results[0]["out"]
```

```python
from contextlib import ExitStack

import concourse.bass as bass
from concourse import mybir

F32 = mybir.dt.float32
BF16 = mybir.dt.bfloat16
I32 = mybir.dt.int32
ALU = mybir.AluOpType
ACT = mybir.ActivationFunctionType
AXX = mybir.AxisListType.X

P = 128
S, L, H = 16, 1024, 256
TOKENS = S * L
DI, NS, R, TAPS = 512, 16, 64, 4
CH = DI // P
KH = H // P
T = 512
TB = T // P
HALVES = L // T
EPS = 1e-5
HEADS, KV, HD = 16, 8, 16
EXPERTS, TOPK, FFN = 8, 2, 1024
CAP = 5120
SLOTS = EXPERTS * CAP


class Allocator:

    def __init__(self, nc, ctx, prefix):
        self.nc, self.ctx, self.prefix = nc, ctx, prefix

    def sb(self, name, shape, dtype=F32):
        return self.ctx.enter_context(self.nc.sbuf_tensor(self.prefix + name, shape, dtype))

    def ps(self, name, shape, dtype=F32):
        return self.ctx.enter_context(self.nc.psum_tensor(self.prefix + name, shape, dtype))

    def sem(self, name):
        return self.ctx.enter_context(self.nc.semaphore(self.prefix + name))


def count(block, per_block, done):
    b, half = block
    return b * (HALVES * per_block) + (half * per_block + done)


def wait(eng, sem, value):
    if isinstance(value, int) and value <= 0:
        return
    eng.wait_ge(sem, value)


def wait_apart(eng, sem, value, passed):
    if isinstance(value, int) and value <= 0:
        return
    eng.wait_ge(sem, value)
    eng.sem_inc(passed, 1)


def mamba_stage(nc, x, w, x1):
    POSITIONS, SIDE_BANKS = NS * CH, 3
    REST = (None, 0, 1)
    SIDE = ([("xnT", 0, 1), ("xnT", 1, 1), ("x", 0, KH), ("x", 1, KH)] + [("y", i, 1) for i in range(CH)]
            + [("conv", 0, TAPS), REST, ("x", 2, KH), ("conv", 1, TAPS), REST, ("x", 3, KH), ("conv", 2, TAPS),
               ("conv", 3, TAPS), ("z", 0, KH), ("dbl", 0, CH), REST, ("dt", 0, 1), ("z", 1, KH),
               ("dt", 1, 1), ("C", 0, 1), ("dt", 2, 1), REST, ("dt", 3, 1), ("out", 0, 4), REST, ("out", 1, 4)]
            + [("z", 2, KH), ("z", 3, KH)] + [("skip", j, 1) for j in range(TB)])
    VECTOR_KINDS = ("y", "out")
    SILU_KINDS = ("conv", "z")
    uses = [(kind, i) for kind, i, _ in SIDE if kind]
    gate_uses = [u for u in uses if u[0] in VECTOR_KINDS]
    prep_uses = [u for u in uses if u[0] not in VECTOR_KINDS]
    GATES, PREPS = len(gate_uses), len(prep_uses)
    pieces_at = {}
    filled_at = {}
    v = 0
    for kind, i, n in SIDE:
        if kind:
            pieces_at.update({v + piece: (kind, i, piece, n) for piece in range(n)})
            filled_at[v + n - 1] = (kind, i)
        v += n
    assert v == POSITIONS and len(uses) % SIDE_BANKS == 0
    position_of = {u: v for v, u in filled_at.items()}
    LN_AT = position_of[("dt", CH - 1)] + 3
    NORMALISE_AT = LN_AT + 7
    DELTA_AT = LN_AT + 2
    REST_AT = position_of["dbl", 0] + 2
    MIDDLE_AT = REST_AT + 1
    LOW_AT = MIDDLE_AT + 1
    COPY_B_AT = [2 if CH * n + 2 in filled_at and CH * n + 1 not in filled_at else 3 for n in range(NS)]

    def prep_done(kind, i):
        return 1 + prep_uses.index((kind, i))

    def gate_done(kind, i):
        return 1 + gate_uses.index((kind, i))

    def bank_of(kind, i):
        return uses.index((kind, i)) % SIDE_BANKS

    with ExitStack() as ctx:
        al = Allocator(nc, ctx, "m_")
        sb, sem = al.sb, al.sem
        w_in = sb("w_in", [P, KH, 2 * DI])
        w_x = sb("w_x", [P, CH, P])
        w_dt = sb("w_dt", [R, DI])
        w_out = sb("w_out", [P, CH, H])
        a_log = sb("a_log", [P, CH, NS])
        a_neg = sb("a_neg", [P, CH, NS])
        conv_w = sb("conv_w", [P, CH, TAPS])
        vecs = sb("vecs", [P, 3, CH])
        half_bias = sb("half_bias", [P, CH])
        ident = sb("ident", [P, P])
        tap_diag = sb("tap_diag", [P, CH, TAPS, P])
        skip_diag = sb("skip_diag", [P, CH, P])
        pick = sb("pick", [R + NS, NS, P], BF16)
        xin = sb("xin", [P, TB, H])
        stats = sb("stats", [P, TB, 6])
        moments = sb("moments", [P, TB, 2])
        rstd = sb("rstd", [P, TB])
        minus_half = sb("minus_half", [P, TB])
        eps = sb("eps", [P, TB])
        xn = sb("xn", [P, TB, H])
        xnT = sb("xnT", [P, KH, T])
        xpad = sb("xpad", [P, CH, TAPS - 1 + T])
        tanh = sb("tanh", [P, 2, T])
        hlf = sb("hlf", [P, 2, T])
        xc = sb("xc", [P, CH, T])
        dbl = sb("dbl", [P, 2, T])
        b_parts = sb("b_parts", [R + NS, 2, T], BF16)
        b_rest = sb("b_rest", [R + NS, T])
        b_middle = sb("b_middle", [R + NS, T], BF16)
        sp_e = sb("sp_e", [P, CH, T])
        sp_r = sb("sp_r", [P, CH, T])
        delta = sb("delta", [P, 2, CH, T])
        du = sb("du", [P, 2, CH, T])
        zs = sb("zs", [P, 2, CH, T])
        cT = sb("cT", [P, 2, TB, NS])
        bb = sb("bb", [P, 2, T])
        dbu = sb("dbu", [P, 2, CH, T])
        h = sb("h", [P, 2, CH, T])
        h_end = sb("h_end", [P, NS, CH])
        acc = sb("acc", [P, 2, TB, DI])
        y = sb("y", [P, CH, T])
        xres = sb("xres", [P, TB, H])
        decay = al.ps("decay", [P, 2, T])
        hT = al.ps("hT", [P, 2, DI])
        bcast = al.ps("bcast", [P, T])
        side_bank = al.ps("side", [P, SIDE_BANKS, T])

        s_weights = sem("weights")
        s_const = sem("const")
        s_a = sem("a")
        s_diag = sem("diag")
        dve_passed, sp_passed = sem("dve_passed"), sem("sp_passed")
        x_loaded = sem("x_loaded")
        xres_loaded = sem("xres_loaded")
        x1_stored = sem("x1_stored")
        stats_done = sem("stats_done")
        rstd_done = sem("rstd_done")
        ln_done = sem("ln_done")
        prep_made = sem("prep_made")
        prep_taken = sem("prep_taken")
        gate_made = sem("gate_made")
        gate_taken = sem("gate_taken")
        halo_done = sem("halo_done")
        tanh_done = sem("tanh_done")
        silu_done = sem("silu_done")
        soft_done = sem("soft_done")
        delta_done = sem("delta_done")
        du_done = sem("du_done")
        rest_done = sem("rest_done")
        middle_done = sem("middle_done")
        parts_done = sem("parts_done")
        bcast_made = sem("bcast_made")
        bb_done = sem("bb_done")
        dbu_done = sem("dbu_done")
        decay_done = sem("decay_done")
        scan_done = sem("scan_done")
        hT_done = sem("hT_done")
        sum_done = sem("sum_done")
        end_saved = sem("end_saved")

        x_blocks = x.rearrange("s (h j p) m -> s h p j m", h=HALVES, p=P)
        x1_blocks = x1.rearrange("s (h j p) m -> s h p j m", h=HALVES, p=P)

        block = ctx.enter_context(nc.Block())

        def before(q):
            return (q[0], q[1] - 1) if q[1] else (q[0] - 1, HALVES - 1)

        def after(q):
            return (q[0], q[1] + 1) if q[1] < HALVES - 1 else (q[0] + 1, 0)

        def first(q):
            return isinstance(q[0], int) and q[0] == 0 and q[1] == 0

        def sequences(eng, body):
            body(0, False)
            with eng.Fori(1, S - 1) as b:
                body(b, False)
            body(S - 1, True)

        @block.sync
        def _(sp):
            def wait_then_address(sem_, value):
                wait_apart(sp, sem_, value, sp_passed)

            def load_x(q):
                if not first(q):
                    wait_then_address(ln_done, count(q, 1, 0))
                sp.dma_start(xin[:], x_blocks[q[0], q[1]]).then_inc(x_loaded, 16)

            def move(q, last):
                if not last:
                    load_x(after(after(q)))
                if not first(q):
                    g = before(q)
                    wait_then_address(x1_stored, count(g, 16, 0))
                    sp.dma_start(xres[:], x_blocks[g[0], g[1]]).then_inc(xres_loaded, 16)
                    wait_then_address(gate_taken, count(g, GATES, GATES))
                    sp.dma_start(x1_blocks[g[0], g[1]], xres[:]).then_inc(x1_stored, 16)

            load_x((0, 0))
            for dst, src in ((w_in[:], w["in_T"].rearrange("(k p) e -> p k e", p=P)),
                             (w_dt[:], w["dt_T"]),
                             (w_out[:], w["out_T"].rearrange("(c p) m -> p c m", p=P)),
                             (a_log[:], w["A_log"].rearrange("(c p) n -> p c n", p=P)),
                             (conv_w[:], w["conv_w"].rearrange("(c p) k -> p c k", p=P)),
                             (vecs[:], w["vecs"].rearrange("v p c -> p v c"))):
                sp.dma_start(dst, src).then_inc(s_weights, 16)
            sp.wait_ge(s_const, 6)
            w_xT = w["x_T"].rearrange("(c p) e -> p c e", p=P)
            sp.dma_start(w_x[:, :, 0:R + NS], w_xT[:, :, 0:R + NS]).then_inc(s_weights, 16)
            sp.dma_start(w_x[:, :, 96:96 + NS], w_xT[:, :, R + NS:R + 2 * NS]).then_inc(s_weights, 16)
            load_x((0, 1))

            def body(b, last):
                for half in range(HALVES):
                    move((b, half), last)
            sequences(sp, body)
            g = (S - 1, HALVES - 1)
            sp.wait_ge(x1_stored, count(g, 16, 0))
            sp.dma_start(xres[:], x_blocks[g[0], g[1]]).then_inc(xres_loaded, 16)
            sp.wait_ge(gate_taken, count(g, GATES, GATES))
            sp.dma_start(x1_blocks[g[0], g[1]], xres[:]).then_inc(x1_stored, 16)
            sp.wait_ge(x1_stored, 16 * S * HALVES)

        @block.gpsimd
        def _(pool):
            nc.gpsimd.memset(minus_half[:], -0.5).then_inc(s_const, 1)
            nc.gpsimd.memset(eps[:], EPS).then_inc(s_const, 1)
            nc.gpsimd.memset(ident[:], 0.0).then_inc(s_const, 1)
            nc.gpsimd.memset(pick[:], 0.0).then_inc(s_const, 1)
            nc.gpsimd.memset(w_x[:], 0.0).then_inc(s_const, 1)
            nc.gpsimd.memset(b_parts[:], 0.0).then_inc(s_const, 1)
            pool.wait_ge(s_const, 6)
            nc.gpsimd.affine_select(out=ident[:], in_=ident[:], compare_op=ALU.not_equal, fill=1.0,
                                    base=0, pattern=[[-1, P]], channel_multiplier=1).then_inc(s_const, 1)
            for part, row in enumerate((0, 32, 64)):
                pool.wait_ge(s_const, 7 + part)
                nc.gpsimd.affine_select(out=pick[:], in_=pick[:], compare_op=ALU.not_equal, fill=1.0,
                                        base=-row, pattern=[[-1, NS], [0, P]], channel_multiplier=1).then_inc(s_const, 1)

            def inverse_deviation(q):
                wait(pool, stats_done, count(q, 2, 2))
                nc.gpsimd.tensor_tensor(rstd[:], moments[:, :, 1], eps[:], ALU.add).then_inc(rstd_done, 1)
                wait(pool, rstd_done, count(q, 2, 1))
                nc.gpsimd.tensor_tensor(rstd[:], rstd[:], minus_half[:], ALU.pow).then_inc(rstd_done, 1)

            def du_part(q, part):
                cs = slice(part * (CH // 2), (part + 1) * (CH // 2))
                wait(pool, delta_done, count(q, CH, (part + 1) * (CH // 2)))
                nc.gpsimd.tensor_tensor(du[:, q[1], cs], delta[:, q[1], cs], xc[:, cs], ALU.mult).then_inc(du_done, 1)

            inverse_deviation((0, 0))
            inverse_deviation((0, 1))
            du_part((0, 0), 0)
            du_part((0, 0), 1)

            def body(b, last):
                for half in range(HALVES):
                    q = (b, half)
                    wait(pool, du_done, count(q, 2, 2))
                    for n in range(NS):
                        wait(pool, bb_done, count(q, NS, n + 1))
                        wait(pool, scan_done, count(q, 4 * NS, 4 * (n - 1)))
                        nc.gpsimd.tensor_tensor(
                            dbu[:, n % 2], du[:, half],
                            bb[:, n % 2].unsqueeze(1).to_broadcast([P, CH, T]),
                            ALU.mult).then_inc(dbu_done, 1)
                        if n == LN_AT // CH + 1 and not last:
                            inverse_deviation(after(after(q)))
                        if n >= NS - 2 and not (last and half == HALVES - 1):
                            du_part(after(q), n - (NS - 2))
            sequences(pool, body)

        @block.scalar
        def _(act):
            act.wait_ge(s_weights, 16 * 8)
            act.wait_ge(s_const, 10)
            nc.scalar.activation(a_neg[:], a_log[:], ACT.Exp).then_inc(s_a, 1)
            nc.scalar.mul(half_bias[:], vecs[:, 0, :], 0.5).then_inc(s_a, 1)
            act.wait_ge(s_a, 1)
            nc.scalar.mul(a_neg[:], a_neg[:], -1.0).then_inc(s_a, 1)
            act.wait_ge(s_a, 3)

            def take(q, kind, i):
                bank = side_bank[:, bank_of(kind, i)]
                r = q[1]
                wait(act, prep_made, count(q, PREPS, prep_done(kind, i)))
                if kind == "xnT":
                    ins = nc.scalar.copy(xnT[:, i], bank)
                elif kind == "x":
                    if i == 0:
                        wait(act, prep_made, count(before(q), PREPS, prep_done("conv", CH - 1)))
                        wait(act, prep_taken, count(before(q), PREPS, prep_done("x", CH - 1)))
                        if r:
                            nc.scalar.copy(xpad[:, :, 0:TAPS - 1], xpad[:, :, T:T + TAPS - 1]).then_inc(halo_done, 1)
                        else:
                            nc.scalar.mul(xpad[:, :, 0:TAPS - 1], ident[:, 0:CH * (TAPS - 1)].rearrange(
                                "p (c k) -> p c k", c=CH), 0.0).then_inc(halo_done, 1)
                        wait(act, halo_done, count(q, 1, 1))
                    ins = nc.scalar.copy(xpad[:, i, TAPS - 1:], bank)
                elif kind in ("conv", "z"):
                    k = i + (CH if kind == "z" else 0)
                    wait(act, silu_done, count(q, 2 * CH, k - 1))
                    bias = half_bias[:, i:i + 1] if kind == "conv" else 0.0
                    nc.scalar.activation(tanh[:, k % 2], bank, ACT.Tanh, scale=0.5, bias=bias)
                    ins = nc.scalar.activation(hlf[:, k % 2], bank, ACT.Identity, scale=0.5, bias=bias)
                elif kind == "dbl":
                    wait(act, bcast_made, count(before(before(q)), NS, NS))
                    nc.scalar.copy(b_parts[R:R + NS, r], bank[R:R + NS])
                    ins = nc.scalar.copy(dbl[:, r], bank)
                elif kind == "dt":
                    if i == 0:
                        wait(act, delta_done, count(q, CH, 0))
                    nc.scalar.activation(sp_e[:, i], bank, ACT.Abs, bias=vecs[:, 1, i:i + 1])
                    ins = nc.scalar.activation(sp_r[:, i], bank, ACT.Relu, bias=vecs[:, 1, i:i + 1])
                elif kind == "C":
                    wait(act, sum_done, count(before(before(q)), 4 * NS, 4 * NS))
                    ins = nc.scalar.copy(cT[:, r], bank.rearrange("p (j e) -> p j e", j=TB)[:, :, 96:96 + NS])
                elif kind == "skip":
                    wait(act, gate_made, count(before(before(q)), GATES, CH))
                    ins = nc.scalar.copy(acc[:, r, i], bank)
                ins.then_inc(prep_taken, 1)

            def softplus_exp(q, i):
                wait(act, prep_taken, count(q, PREPS, prep_done("dt", i)))
                nc.scalar.activation(sp_e[:, i], sp_e[:, i], ACT.Exp, scale=-1.0).then_inc(soft_done, 1)

            def softplus_ln(q):
                wait(act, soft_done, count(q, CH + 1, CH))
                nc.scalar.activation(sp_e[:], sp_e[:], ACT.Ln, bias=1.0).then_inc(soft_done, 1)

            def prepare(q, v):
                if v - 2 in filled_at and filled_at[v - 2][0] in SILU_KINDS:
                    take(q, *filled_at[v - 2])
                if v - 1 in filled_at and filled_at[v - 1] in prep_uses and filled_at[v - 1][0] not in SILU_KINDS:
                    take(q, *filled_at[v - 1])
                if v - 2 in filled_at and filled_at[v - 2][0] == "dt":
                    softplus_exp(q, filled_at[v - 2][1])
                if v == LN_AT:
                    softplus_ln(q)
                if v == MIDDLE_AT:
                    wait(act, rest_done, count(q, 1, 1))
                    for dst in (b_middle[R:R + NS], b_parts[32:32 + NS, q[1]]):
                        nc.scalar.copy(dst, b_rest[R:R + NS]).then_inc(middle_done, 1)

            for v in range(POSITIONS + 1):
                prepare((0, 0), v)

            def copy_b(q, n):
                wait(act, bcast_made, count(q, NS, n + 1))
                wait(act, dbu_done, count(q, NS, n - 1))
                nc.scalar.copy(bb[:, n % 2], bcast[:]).then_inc(bb_done, 1)

            copy_b((0, 0), 0)
            copy_b((0, 0), 1)

            def scan_block(q, last):
                r = q[1]
                wait(act, delta_done, count(q, CH, CH))
                for n in range(NS):
                    for c in range(CH):
                        wait(act, scan_done, count(q, 4 * NS, 4 * n + c - 1))
                        nc.scalar.activation(decay[:, c % 2], delta[:, r, c], ACT.Exp,
                                             scale=a_neg[:, c, n:n + 1]).then_inc(decay_done, 1)
                        if not last:
                            prepare(after(q), CH * n + c)
                        if c == COPY_B_AT[n]:
                            if n + 2 < NS:
                                copy_b(q, n + 2)
                            elif not last:
                                copy_b(after(q), n + 2 - NS)
                if not last:
                    prepare(after(q), POSITIONS)

            def body(b, last):
                for half in range(HALVES):
                    scan_block((b, half), last and half == HALVES - 1)
            sequences(act, body)

        @block.vector
        def _(dve):
            dve.wait_ge(s_weights, 16 * 8)
            dve.wait_ge(s_const, 10)
            for c in range(CH):
                for k in range(TAPS):
                    nc.vector.tensor_scalar(tap_diag[:, c, k], ident[:], conv_w[:, c, k:k + 1], None, ALU.mult)
                ins = nc.vector.tensor_scalar(skip_diag[:, c], ident[:], vecs[:, 2, c:c + 1], None, ALU.mult)
            ins.then_inc(s_diag, 1)

            def statistics(q):
                wait(dve, x_loaded, count(q, 16, 16))
                for j in range(TB):
                    ins = nc.vector.bn_stats(stats[:, j], xin[:, j])
                ins.then_inc(stats_done, 1)
                wait_apart(dve, stats_done, count(q, 2, 1), dve_passed)
                for j in range(TB):
                    ins = nc.vector.bn_aggr(moments[:, j], stats[:, j])
                ins.then_inc(stats_done, 1)

            def normalise(q, part):
                if part == 0:
                    wait(dve, rstd_done, count(q, 2, 2))
                    wait(dve, prep_made, count(before(q), PREPS, prep_done("xnT", 1)))
                for j in range(2 * part, 2 * part + 2):
                    ins = nc.vector.tensor_scalar(xn[:, j], xin[:, j], moments[:, j, 0:1], rstd[:, j:j + 1],
                                                  ALU.subtract, ALU.mult)
                if part:
                    ins.then_inc(ln_done, 1)

            def silu(q, kind, i):
                k = i + (CH if kind == "z" else 0)
                wait(dve, prep_taken, count(q, PREPS, prep_done(kind, i)))
                if kind == "conv" and i == 0:
                    wait(dve, prep_made, count(before(q), PREPS, prep_done("skip", TB - 1)))
                    wait(dve, du_done, count(before(q), 2, 2))
                if kind == "z" and i == 0:
                    wait(dve, gate_taken, count(before(before(q)), GATES, CH))
                out = xc[:, i] if kind == "conv" else zs[:, q[1], i]
                nc.vector.scalar_tensor_tensor(out=out, in0=tanh[:, k % 2], scalar=1.0, in1=hlf[:, k % 2],
                                               op0=ALU.add, op1=ALU.mult).then_inc(silu_done, 1)

            def gate(q, kind, i):
                wait(dve, gate_made, count(q, GATES, gate_done(kind, i)))
                bank = side_bank[:, bank_of(kind, i)]
                if kind == "y":
                    if i == 0:
                        wait(dve, gate_made, count(before(q), GATES, GATES))
                    nc.vector.tensor_tensor(y[:, i], bank, zs[:, q[1], i], ALU.mult).then_inc(gate_taken, 1)
                else:
                    if i == 0:
                        wait(dve, xres_loaded, count(q, 16, 16))
                    nc.vector.tensor_tensor(xres[:, 2 * i:2 * i + 2], bank.rearrange("p (j m) -> p j m", j=2),
                                            xres[:, 2 * i:2 * i + 2], ALU.add).then_inc(gate_taken, 1)

            def side_work(q, v, gates, preps, norm):
                if gates and filled_at.get(v - 1) in gate_uses:
                    gate(before(q), *filled_at[v - 1])
                if not preps:
                    return
                p = after(q)
                if v == LN_AT and norm:
                    statistics(after(p))
                if v == REST_AT:
                    wait(dve, prep_taken, count(p, PREPS, prep_done("dbl", 0)))
                    nc.vector.tensor_tensor(b_rest[R:R + NS], dbl[R:R + NS, p[1]], b_parts[R:R + NS, p[1]],
                                            ALU.subtract).then_inc(rest_done, 1)
                if v == LOW_AT:
                    wait(dve, middle_done, count(p, 2, 2))
                    nc.vector.tensor_tensor(b_parts[0:NS, p[1]], b_rest[R:R + NS], b_middle[R:R + NS],
                                            ALU.subtract).then_inc(parts_done, 1)
                if v - NORMALISE_AT in (0, 1) and norm:
                    normalise(after(p), v - NORMALISE_AT)
                if v - 3 in filled_at and filled_at[v - 3][0] in SILU_KINDS:
                    silu(p, *filled_at[v - 3])
                if DELTA_AT <= v < DELTA_AT + CH:
                    c = v - DELTA_AT
                    wait(dve, soft_done, count(p, CH + 1, CH + 1))
                    nc.vector.tensor_tensor(delta[:, p[1], c], sp_e[:, c], sp_r[:, c], ALU.add).then_inc(delta_done, 1)

            def prologue():
                statistics((0, 0))
                normalise((0, 0), 0)
                normalise((0, 0), 1)
                for v in range(POSITIONS):
                    side_work((-1, 1), v, False, True, True)
            prologue()

            def add_state(q, n, j):
                wait(dve, hT_done, count(q, 4 * NS, 4 * n + j + 1))
                if n == 0:
                    wait(dve, prep_taken, count(q, PREPS, prep_done("skip", j)))
                else:
                    wait(dve, sum_done, count(q, 4 * NS, 4 * n + j - 3))
                nc.vector.scalar_tensor_tensor(out=acc[:, q[1], j], in0=hT[:, j % 2], scalar=cT[:, q[1], j, n:n + 1],
                                               in1=acc[:, q[1], j], op0=ALU.mult, op1=ALU.add).then_inc(sum_done, 1)

            def scan_block(q, last, norm):
                r = q[1]
                for n in range(NS):
                    for c in range(CH):
                        wait(dve, decay_done, count(q, 4 * NS, 4 * n + c + 1))
                        if c == 0:
                            wait(dve, dbu_done, count(q, NS, n + 1))
                            wait(dve, hT_done, count(q, 4 * NS, 4 * (n - 1)))
                            if r:
                                wait(dve, end_saved, q[0] * NS + (n + 1))
                        nc.vector.tensor_tensor_scan(h[:, n % 2, c], decay[:, c % 2], dbu[:, n % 2, c],
                                                     h_end[:, n, c:c + 1] if r else 0.0,
                                                     ALU.mult, ALU.add).then_inc(scan_done, 1)
                        if n:
                            add_state(q, n - 1, c)
                        elif not first(q):
                            add_state(before(q), NS - 1, c)
                        side_work(q, CH * n + c, not first(q), not last, norm)
                    if not r:
                        wait(dve, scan_done, count(q, 4 * NS, 4 * (n + 1)))
                        nc.vector.tensor_copy(h_end[:, n], h[:, n % 2, :, T - 1]).then_inc(end_saved, 1)

            def body(b, last):
                for half in range(HALVES):
                    scan_block((b, half), last and half == HALVES - 1, not last)
            sequences(dve, body)
            q = (S - 1, HALVES - 1)
            for j in range(TB):
                add_state(q, NS - 1, j)
            for use in gate_uses:
                gate(q, *use)

        @block.tensor
        def _(pe):
            pe.wait_ge(s_diag, 1)
            pe.wait_ge(s_const, 10)
            pe.wait_ge(s_weights, 16 * 8)

            def bank_free(q, use, gates, preps):
                k = uses.index(use) - SIDE_BANKS
                while k >= 0 and not (gates if uses[k] in gate_uses else preps):
                    k -= SIDE_BANKS
                if k < 0:
                    wait(pe, prep_taken, count(q, PREPS, PREPS + k + 1))
                elif uses[k] in gate_uses:
                    wait(pe, gate_taken, count(before(q), GATES, gate_done(*uses[k])))
                else:
                    wait(pe, prep_taken, count(after(q), PREPS, prep_done(*uses[k])))

            def piece_of_work(q, v, gates, preps):
                if v not in pieces_at:
                    return
                kind, i, piece, pieces = pieces_at[v]
                if not (gates if kind in VECTOR_KINDS else preps):
                    return
                if piece == 0:
                    bank_free(q, (kind, i), gates, preps)
                fill(before(q) if kind in VECTOR_KINDS else after(q), kind, i, piece, pieces)

            def fill(p, kind, i, piece, pieces):
                bank = side_bank[:, bank_of(kind, i)]
                final = piece == pieces - 1
                if kind == "y":
                    if i == 0:
                        wait(pe, sum_done, count(p, 4 * NS, 4 * NS))
                    for j in range(TB):
                        ins = nc.tensor.transpose(bank[:, j * P:(j + 1) * P],
                                                  acc[:, p[1], j, i * P:(i + 1) * P], ident[:])
                elif kind == "out":
                    if piece == 0:
                        wait(pe, gate_taken, count(p, GATES, CH))
                    j, part = piece // 2, piece % 2
                    t = (2 * i + j) * P
                    for c in range(part * (CH // 2), (part + 1) * (CH // 2)):
                        ins = nc.tensor.matmul(bank[:, j * H:(j + 1) * H], y[:, c, t:t + P], w_out[:, c],
                                               start=(c == 0), stop=(c == CH - 1))
                elif kind == "xnT":
                    if i == 0:
                        wait(pe, ln_done, count(p, 1, 1))
                    for j in range(TB):
                        ins = nc.tensor.transpose(bank[:, j * P:(j + 1) * P], xn[:, j, i * P:(i + 1) * P], ident[:])
                elif kind in ("x", "z"):
                    col = i * P + (DI if kind == "z" else 0)
                    if piece == 0:
                        wait(pe, prep_taken, count(p, PREPS, prep_done("xnT", KH - 1)))
                    ins = nc.tensor.matmul(bank, w_in[:, piece, col:col + P], xnT[:, piece],
                                           start=(piece == 0), stop=final)
                elif kind == "conv":
                    if piece == 0:
                        wait(pe, prep_taken, count(p, PREPS, prep_done("x", i)))
                    ins = nc.tensor.matmul(bank, tap_diag[:, i, piece], xpad[:, i, piece:piece + T],
                                           start=(piece == 0), stop=final)
                elif kind == "dbl":
                    wait(pe, silu_done, count(p, 2 * CH, piece + 1))
                    ins = nc.tensor.matmul(bank, w_x[:, piece], xc[:, piece], start=(piece == 0), stop=final)
                elif kind == "dt":
                    if i == 0:
                        wait(pe, prep_taken, count(p, PREPS, prep_done("dbl", 0)))
                    ins = nc.tensor.matmul(bank, w_dt[:, i * P:(i + 1) * P], dbl[0:R, p[1]], start=True, stop=True)
                elif kind == "C":
                    for j in range(TB):
                        ins = nc.tensor.transpose(bank[:, j * P:(j + 1) * P], dbl[:, p[1], j * P:(j + 1) * P], ident[:])
                elif kind == "skip":
                    for c in range(CH):
                        ins = nc.tensor.matmul(bank[:, c * P:(c + 1) * P], xc[:, c, i * P:(i + 1) * P],
                                               skip_diag[:, c], start=True, stop=True)
                if final:
                    ins.then_inc(gate_made if kind in VECTOR_KINDS else prep_made, 1)

            for v in range(POSITIONS):
                piece_of_work((-1, 1), v, False, True)

            def spread_b(q, n):
                wait(pe, bb_done, count(q, NS, n))
                if n == 0:
                    wait(pe, parts_done, count(q, 1, 1))
                nc.tensor.matmul(bcast[:], pick[:, n], b_parts[:, q[1]],
                                 start=True, stop=True).then_inc(bcast_made, 1)

            spread_b((0, 0), 0)
            spread_b((0, 0), 1)

            def turn(q, n, j):
                if j == 0:
                    wait(pe, scan_done, count(q, 4 * NS, 4 * (n + 1)))
                wait(pe, sum_done, count(q, 4 * NS, 4 * n + j - 1))
                for c in range(CH):
                    ins = nc.tensor.transpose(hT[:, j % 2, c * P:(c + 1) * P], h[:, n % 2, c, j * P:(j + 1) * P],
                                              ident[:])
                ins.then_inc(hT_done, 1)

            def scan_block(q, last):
                gates, preps = not first(q), not last
                for n in range(NS):
                    for j in range(TB):
                        if n:
                            turn(q, n - 1, j)
                        elif not first(q):
                            turn(before(q), NS - 1, j)
                        piece_of_work(q, CH * n + j, gates, preps)
                        if j == 1:
                            if n + 2 < NS:
                                spread_b(q, n + 2)
                            elif not last:
                                spread_b(after(q), n + 2 - NS)

            def body(b, last):
                for half in range(HALVES):
                    scan_block((b, half), last and half == HALVES - 1)
            sequences(pe, body)
            q = (S - 1, HALVES - 1)
            for j in range(TB):
                turn(q, NS - 1, j)
            wait(pe, gate_taken, count(before(q), GATES, GATES))
            for k, (kind, i) in enumerate(gate_uses):
                same = [g for g in gate_uses[:k] if bank_of(*g) == bank_of(kind, i)]
                if same:
                    wait(pe, gate_taken, count(q, GATES, gate_done(*same[-1])))
                pieces = dict((u[:2], u[2]) for u in SIDE)[kind, i]
                for piece in range(pieces):
                    fill(q, kind, i, piece, pieces)


def attention_stage(nc, x1, w, base, n2, logits, slot_rows, slot_out):
    PLACES = P
    BLOCKS = L // PLACES
    GL = 16
    GROUPS = PLACES // GL
    PAIR = HEADS // KV
    LN1_GROUP, LN2_GROUP = 1, 4
    POOL_SPREADS = (2, 4, 5, 7)
    VECTOR_SPREADS = [i for i in range(GROUPS) if i not in POOL_SPREADS]
    NORM_T, PROJ, QKV, NORM2_T = 8, 8, 16, 8
    MADE, ACT_TAKES = NORM_T + PROJ + QKV + NORM2_T, NORM_T + QKV + NORM2_T

    with ExitStack() as ctx:
        al = Allocator(nc, ctx, "a_")
        sb, sem = al.sb, al.sem
        w_qkv = sb("w_qkv", [P, KH, 4 * P])
        w_proj = sb("w_proj", [P, PAIR, H])
        w_router = sb("w_router", [P, KH, EXPERTS])
        ln_vecs = sb("ln_vecs", [P, 4, KH])
        ident = sb("ident", [P, P])
        head_mask = sb("head_mask", [P, KV])
        causal = sb("causal", [P, NS])
        s_of_p = sb("s_of_p", [P, NS])
        row_i = sb("row_i", [P, NS], I32)
        col_i = sb("col_i", [P, NS], I32)
        minus_half = sb("minus_half", [P, S])
        eps = sb("eps", [P, S])
        xa = sb("xa", [P, S, H])
        zeros = sb("zeros", [P, 2048])
        u = sb("u", [P, 2, S, H])
        stats = sb("stats", [P, S, 6])
        moments = sb("moments", [P, S, 2])
        rstd = sb("rstd", [P, S])
        n1 = sb("n1", [P, S, H])
        n2_sb = sb("n2", [P, S, H])
        oT = n2_sb[:].rearrange("p (a s) m -> p a (s m)", a=PAIR).rearrange("p a (s l) -> p a s l", s=S)
        xT = sb("xT", [P, KH, S, P])
        qT = sb("qT", [P, PAIR, S, P])
        kT = sb("kT", [P, S, P])
        vT = sb("vT", [P, S, P])
        kx = sb("kx", [P, 2, GL, KV, S])
        vx = sb("vx", [P, 2, GL, KV, S])
        vbd = sb("vbd", [P, 2, GL, P])
        sm = sb("sm", [P, 2, 4 * KV, S])
        mx = sb("mx", [P, 2, 4 * KV])
        pT = sb("pT", [P, 2, 4 * P])
        o_rows = sb("o_rows", [P, 2, 4 * P])
        lg = sb("lg", [P, S, EXPERTS])
        common = al.ps("common", [P, 2, 512])
        score = al.ps("score", [P, 2, 512])
        vbank = al.ps("vbank", [P, 2, 512])
        pbank = al.ps("pbank", [P, 512])
        obank = al.ps("obank", [P, 512])

        s_w = sem("weights")
        s_const = sem("const")
        zeroed, cleared = sem("zeroed"), sem("cleared")
        mask_step = sem("mask_step")
        x_loaded = sem("x_loaded")
        base_stored = sem("base_stored")
        n2_stored = sem("n2_stored")
        lg_stored = sem("lg_stored")
        moments_done = sem("moments_done")
        rstd_done = sem("rstd_done")
        u_done = sem("u_done")
        n1_done = sem("n1_done")
        made = sem("made")
        act_took = sem("act_took")
        dve_took = sem("dve_took")
        kx_done = sem("kx_done")
        vx_by_vector = sem("vx_by_vector")
        vx_by_pool = sem("vx_by_pool")
        score_made = sem("score_made")
        vbank_made = sem("vbank_made")
        vbd_done = sem("vbd_done")
        soft = sem("soft")
        exp_done = sem("exp_done")
        pbank_made = sem("pbank_made")
        pbank_took = sem("pbank_took")
        obank_made = sem("obank_made")
        rows_done = sem("rows_done")
        turned = sem("turned")
        o_done = sem("o_done")
        base_done = sem("base_done")
        n2_done = sem("n2_done")
        dve_passed, sp_passed, act_passed = sem("dve_passed"), sem("sp_passed"), sem("act_passed")

        x1_b = x1.rearrange("s (b p) m -> b p s m", p=P)
        base_b = base.rearrange("s (b p) m -> b p s m", p=P)
        n2_b = n2.rearrange("s (b p) m -> b p s m", p=P)

        block = ctx.enter_context(nc.Block())

        def at(b, per_block, done):
            if isinstance(b, int):
                return b * per_block + done
            return b[0] * (2 * per_block) + ((1 + b[1]) * per_block + done)

        def parity(b):
            return b % 2 if isinstance(b, int) else (1 + b[1]) % 2

        def is_last(b):
            return isinstance(b, int) and b == BLOCKS - 1

        def blocks(eng, body):
            body(0)
            with eng.Fori(0, (BLOCKS - 2) // 2) as pair:
                for sub in range(2):
                    body((pair, sub))
            body(BLOCKS - 1)

        def front_count(b, per_front, per_round, done):
            return done if isinstance(b, int) and b == -1 else at(b, per_round, per_front + done)

        def made_at(b, done):
            return front_count(b, NORM_T + QKV, MADE, done)

        def took_at(b, done):
            return front_count(b, NORM_T + QKV, ACT_TAKES, done)

        def ln_at(b, done):
            return front_count(b, 4, 6, done)

        def common_use(b, kind, k):
            fronts = 0 if is_last(b) else 1
            alone = isinstance(b, int) and b == -1
            if kind == "norm":
                return made_at(b, k + 1), act_took, took_at(b, k + 1)
            if kind == "proj":
                return made_at(b, fronts * NORM_T + k + 1), dve_took, at(b, PROJ, k + 1)
            if kind == "qkv":
                return (made_at(b, NORM_T + (0 if alone else PROJ) + k + 1), act_took,
                        took_at(b, NORM_T + k + 1))
            return (made_at(b, fronts * (NORM_T + QKV) + PROJ + k + 1), act_took,
                    took_at(b, fronts * (NORM_T + QKV) + k + 1))

        def qkv_taken(b):
            return NORM_T + QKV if isinstance(b, int) and b == 0 else took_at(b, -NORM2_T)

        def spread_values(eng, b, i):
            wait(eng, vbank_made, at(b, 4 * GROUPS, 4 * (i - 1)))
            eng.tensor_tensor(
                vx[:, i % 2],
                vT[:, :, i * GL:(i + 1) * GL].rearrange("p s l -> p l s").unsqueeze(2).to_broadcast([P, GL, KV, S]),
                head_mask[:].unsqueeze(1).unsqueeze(3).to_broadcast([P, GL, KV, S]),
                ALU.mult).then_inc(vx_by_pool if i in POOL_SPREADS else vx_by_vector, 1)

        @block.sync
        def _(sp):
            for dst, src in ((w_qkv[:], w["qkv_T"].rearrange("(k p) e -> p k e", p=P)),
                             (w_proj[:], w["proj_T"].rearrange("(a p) m -> p a m", p=P)),
                             (w_router[:], w["router"].rearrange("(k p) e -> p k e", p=P)),
                             (ln_vecs[:], w["ln_vecs"])):
                sp.dma_start(dst, src).then_inc(s_w, 16)

            def clear():
                sp.wait_ge(zeroed, 1)
                for dst in (slot_rows, slot_out[SLOTS:SLOTS + P, :]):
                    flat = dst.rearrange("(p r) m -> p (r m)", p=P)
                    size = flat.shape[1]
                    n = size // 2048
                    if n:
                        sp.dma_start(flat[:, 0:n * 2048].rearrange("p (n c) -> p n c", n=n),
                                     zeros[:].unsqueeze(1).to_broadcast([P, n, 2048])).then_inc(cleared, 16)
                    if size - n * 2048:
                        sp.dma_start(flat[:, n * 2048:], zeros[:, 0:size - n * 2048]).then_inc(cleared, 16)

            sp.dma_start(xa[:], x1_b[0]).then_inc(x_loaded, 16)

            def body(b):
                if not is_last(b):
                    wait_apart(sp, u_done if b == 0 else base_stored, 1 if b == 0 else at(b, 16, 0), sp_passed)
                    sp.dma_start(xa[:], x1_b[at(b, 1, 1)]).then_inc(x_loaded, 16)
                    wait_apart(sp, u_done, at(b, 1, 2), sp_passed)
                else:
                    wait_apart(sp, base_stored, at(b, 16, 0), sp_passed)
                sp.dma_start(xa[:], x1_b[at(b, 1, 0)]).then_inc(x_loaded, 16)
                if b == 0:
                    clear()
                wait_apart(sp, base_done, at(b, 1, 1), sp_passed)
                sp.dma_start(base_b[at(b, 1, 0)], xa[:]).then_inc(base_stored, 16)
                wait_apart(sp, n2_done, at(b, 1, 1), sp_passed)
                sp.dma_start(n2_b[at(b, 1, 0)], n2_sb[:]).then_inc(n2_stored, 16)
            blocks(sp, body)
            for done in (base_stored, n2_stored):
                sp.wait_ge(done, 16 * BLOCKS)
            sp.wait_ge(cleared, 16 * 3)

        @block.gpsimd
        def _(pool):
            nc.gpsimd.memset(zeros[:], 0.0).then_inc(zeroed, 1)
            nc.gpsimd.memset(minus_half[:], -0.5).then_inc(s_const, 1)
            nc.gpsimd.memset(eps[:], EPS).then_inc(s_const, 1)
            nc.gpsimd.memset(ident[:], 0.0).then_inc(s_const, 1)
            nc.gpsimd.memset(head_mask[:], 1.0).then_inc(s_const, 1)
            nc.gpsimd.iota(row_i[:], pattern=[[0, NS]], base=0, channel_multiplier=1).then_inc(s_const, 1)
            nc.gpsimd.iota(col_i[:], pattern=[[1, NS]], base=0, channel_multiplier=0).then_inc(s_const, 1)
            pool.wait_ge(s_const, 6)
            nc.gpsimd.affine_select(out=ident[:], in_=ident[:], compare_op=ALU.not_equal, fill=1.0,
                                    base=0, pattern=[[-1, P]], channel_multiplier=1).then_inc(s_const, 1)
            nc.gpsimd.affine_select(out=head_mask[:], in_=head_mask[:], compare_op=ALU.is_ge, fill=0.0,
                                    base=0, pattern=[[-HD, KV]], channel_multiplier=1).then_inc(s_const, 1)
            pool.wait_ge(s_const, 8)
            nc.gpsimd.affine_select(out=head_mask[:], in_=head_mask[:], compare_op=ALU.is_ge, fill=0.0,
                                    base=HD - 1, pattern=[[HD, KV]], channel_multiplier=-1).then_inc(s_const, 1)

            def inverse_deviation(b, k):
                k = 0 if is_last(b) else k
                wait(pool, moments_done, ln_at(b, 2 * k + 2))
                nc.gpsimd.tensor_tensor(rstd[:], moments[:, :, 1], eps[:], ALU.add).then_inc(rstd_done, 1)
                wait(pool, rstd_done, ln_at(b, 2 * k + 1))
                nc.gpsimd.tensor_tensor(rstd[:], rstd[:], minus_half[:], ALU.pow).then_inc(rstd_done, 1)

            inverse_deviation(-1, 0)
            inverse_deviation(-1, 1)

            def body(b):
                wait(pool, act_took, qkv_taken(b))
                for i in range(GROUPS):
                    wait(pool, score_made, at(b, GROUPS, i - 1))
                    nc.gpsimd.tensor_tensor(
                        kx[:, i % 2],
                        kT[:, :, i * GL:(i + 1) * GL].rearrange("p s l -> p l s").unsqueeze(2).to_broadcast([P, GL, KV, S]),
                        head_mask[:].unsqueeze(1).unsqueeze(3).to_broadcast([P, GL, KV, S]),
                        ALU.mult).then_inc(kx_done, 1)
                    if i in POOL_SPREADS:
                        spread_values(pool, b, i)
                    if i in (LN1_GROUP + 1, LN2_GROUP + 1) and not is_last(b):
                        inverse_deviation(b, 0 if i == LN1_GROUP + 1 else 1)
                wait(pool, x_loaded, at(b, 32, 32 if is_last(b) else 48))
                wait(pool, dve_took, at(b, PROJ, PROJ))
                nc.gpsimd.tensor_tensor(xa[:], xa[:], u[:, parity(b)], ALU.add).then_inc(base_done, 1)
                inverse_deviation(b, 2)
            blocks(pool, body)

        @block.scalar
        def _(act):
            act.wait_ge(s_w, 16 * 4)

            def take_norm(b, kind, k4, row):
                k, t4 = k4 // 4, k4 % 4
                wait(act, made, common_use(b, kind, k4)[0])
                nc.scalar.activation(xT[:, k, 4 * t4:4 * t4 + 4].rearrange("p s l -> p (s l)"),
                                     common[:, k4 % 2], ACT.Identity,
                                     scale=ln_vecs[:, row, k:k + 1], bias=ln_vecs[:, row + 1, k:k + 1]).then_inc(act_took, 1)

            def take_qkv(b):
                for n in range(QKV):
                    m, t4 = n // 4, n % 4
                    wait(act, made, common_use(b, "qkv", n)[0])
                    dst = (qT[:, 0], qT[:, 1], kT[:], vT[:])[m][:, 4 * t4:4 * t4 + 4].rearrange("p s l -> p (s l)")
                    nc.scalar.activation(dst, common[:, n % 2], ACT.Copy,
                                         scale=HD ** -0.5 if m < 2 else 1.0).then_inc(act_took, 1)

            for k4 in range(NORM_T):
                take_norm(-1, "norm", k4, 0)
            take_qkv(-1)

            def body(b):
                def take_values(i, ks):
                    for k in ks:
                        wait(act, vbank_made, at(b, 4 * GROUPS, 4 * i + k + 1))
                        if k == 0:
                            wait(act, obank_made, at(b, GROUPS, i - 1))
                        nc.scalar.copy(vbd[:, i % 2, 4 * k:4 * k + 4].rearrange("p l d -> p (l d)"),
                                       vbank[:, k % 2]).then_inc(vbd_done, 1)

                def take_probs(i):
                    wait(act, pbank_made, at(b, GROUPS + 1, i + 1))
                    wait(act, obank_made, at(b, GROUPS, i - 1))
                    nc.scalar.copy(pT[:, i % 2], pbank[:]).then_inc(pbank_took, 1)

                def take_rows(i):
                    wait(act, obank_made, at(b, GROUPS, i + 1))
                    wait(act, turned, at(b, GROUPS, i - 1))
                    nc.scalar.copy(o_rows[:, i % 2], obank[:]).then_inc(rows_done, 1)

                for i in range(GROUPS):
                    if i:
                        take_probs(i - 1)
                    take_values(i, (0, 1))
                    wait(act, soft, at(b, 6 * GROUPS, 6 * i + 3))
                    nc.scalar.activation(sm[:, i % 2], sm[:, i % 2], ACT.Exp).then_inc(exp_done, 1)
                    take_values(i, (2, 3))
                    if i:
                        take_rows(i - 1)
                take_probs(GROUPS - 1)
                take_rows(GROUPS - 1)
                if not is_last(b):
                    for k4 in range(NORM_T):
                        take_norm(b, "norm", k4, 0)
                    take_qkv(b)
                for k4 in range(NORM2_T):
                    take_norm(b, "norm2", k4, 2)
                wait(act, pbank_made, at(b, GROUPS + 1, GROUPS + 1))
                wait(act, lg_stored, at(b, 16, 0))
                nc.scalar.copy(lg[:].rearrange("p s e -> p (s e)"), pbank[:, 0:S * EXPERTS]).then_inc(pbank_took, 1)
                wait_apart(act, pbank_took, at(b, GROUPS + 1, GROUPS + 1), act_passed)
                nc.scalar.dma_start(logits[at(b, 1, 0)], lg[:]).then_inc(lg_stored, 16)
            blocks(act, body)
            act.wait_ge(lg_stored, 16 * BLOCKS)

        @block.vector
        def _(dve):
            dve.wait_ge(s_const, 9)
            nc.vector.tensor_single_scalar(row_i[:], row_i[:], S - 1, op=ALU.bitwise_and).then_inc(mask_step, 1)
            nc.vector.tensor_copy(causal[:], col_i[:]).then_inc(mask_step, 1)
            dve.wait_ge(mask_step, 2)
            nc.vector.tensor_copy(s_of_p[:], row_i[:]).then_inc(mask_step, 1)
            dve.wait_ge(mask_step, 3)
            nc.vector.tensor_tensor(causal[:], causal[:], s_of_p[:], ALU.is_gt).then_inc(mask_step, 1)
            dve.wait_ge(mask_step, 4)
            nc.vector.tensor_scalar(causal[:], causal[:], -1.0e9, None, ALU.mult).then_inc(mask_step, 1)
            dve.wait_ge(mask_step, 5)

            def moments_of(b, src, k):
                k = 0 if is_last(b) else k
                for s in range(S):
                    ins = nc.vector.bn_stats(stats[:, s], src[:, s])
                ins.then_inc(moments_done, 1)
                wait_apart(dve, moments_done, ln_at(b, 2 * k + 1), dve_passed)
                for s in range(S):
                    ins = nc.vector.bn_aggr(moments[:, s], stats[:, s])
                ins.then_inc(moments_done, 1)

            def normalise(b, dst, src, k, done):
                k = 0 if is_last(b) else k
                wait(dve, rstd_done, ln_at(b, 2 * k + 2))
                for s in range(S):
                    ins = nc.vector.tensor_scalar(dst[:, s], src[:, s], moments[:, s, 0:1], rstd[:, s:s + 1],
                                                  ALU.subtract, ALU.mult)
                ins.then_inc(done, 1)

            def front(b, step):
                alone = isinstance(b, int) and b == -1
                u_next = u[:, 0 if alone else 1 - parity(b)]
                if step == 0:
                    wait(dve, x_loaded, 16 if alone else at(b, 32, 32))
                    moments_of(b, xa, 0)
                elif step == 1:
                    normalise(b, u_next, xa, 0, u_done)
                elif step == 2:
                    wait(dve, u_done, 1 if alone else at(b, 1, 2))
                    moments_of(b, u_next, 1)
                else:
                    normalise(b, n1, u_next, 1, n1_done)

            for step in range(4):
                front(-1, step)

            def body(b):
                u_b = u[:, parity(b)]
                wait(dve, act_took, qkv_taken(b))

                def softmax_before(i):
                    x = sm[:, i % 2]
                    wait(dve, score_made, at(b, GROUPS, i + 1))
                    wait(dve, pbank_made, at(b, GROUPS + 1, i - 1))
                    nc.vector.tensor_tensor(x, score[:, i % 2].rearrange("p (g t) -> p g t", t=S),
                                            causal[:].unsqueeze(1).to_broadcast([P, 4 * KV, S]), ALU.add).then_inc(soft, 1)
                    wait(dve, soft, at(b, 6 * GROUPS, 6 * i + 1))
                    nc.vector.reduce_max(mx[:, i % 2], x, axis=AXX).then_inc(soft, 1)
                    wait(dve, soft, at(b, 6 * GROUPS, 6 * i + 2))
                    nc.vector.tensor_tensor(x, x, mx[:, i % 2].unsqueeze(2).to_broadcast([P, 4 * KV, S]),
                                            ALU.subtract).then_inc(soft, 1)

                def softmax_after(i):
                    x = sm[:, i % 2]
                    wait(dve, exp_done, at(b, GROUPS, i + 1))
                    nc.vector.reduce_sum(mx[:, i % 2], x, axis=AXX).then_inc(soft, 1)
                    wait(dve, soft, at(b, 6 * GROUPS, 6 * i + 4))
                    nc.vector.reciprocal(mx[:, i % 2], mx[:, i % 2]).then_inc(soft, 1)
                    wait(dve, soft, at(b, 6 * GROUPS, 6 * i + 5))
                    nc.vector.tensor_tensor(x, x, mx[:, i % 2].unsqueeze(2).to_broadcast([P, 4 * KV, S]),
                                            ALU.mult).then_inc(soft, 1)

                def take_output(i):
                    wait(dve, turned, at(b, GROUPS, i + 1))
                    if i == 0:
                        if b != 0:
                            wait(dve, made, made_at(b, 0))
                            wait(dve, n2_stored, at(b, 16, 0))
                    nc.vector.tensor_copy(
                        oT[:, :, :, i * GL:(i + 1) * GL].rearrange("p a s l -> p l (a s)"),
                        pbank[:].rearrange("p (l r) -> p l r", l=GL)).then_inc(o_done, 1)

                spread_values(dve, b, 0)
                front_step = {LN1_GROUP: 0, LN1_GROUP + 2: 1, LN2_GROUP: 2, LN2_GROUP + 2: 3}
                for i in range(GROUPS):
                    if i >= 3:
                        take_output(i - 3)
                    softmax_before(i)
                    if i + 1 in VECTOR_SPREADS:
                        spread_values(dve, b, i + 1)
                    if i in front_step and not is_last(b):
                        front(b, front_step[i])
                    softmax_after(i)
                for i in range(GROUPS - 3, GROUPS):
                    take_output(i)
                for i in range(PROJ):
                    wait(dve, made, common_use(b, "proj", i)[0])
                    nc.vector.tensor_tensor(u_b[:, 2 * i:2 * i + 2], common[:, i % 2].rearrange("p (j m) -> p j m", j=2),
                                            u_b[:, 2 * i:2 * i + 2], ALU.add).then_inc(dve_took, 1)
                wait(dve, dve_took, at(b, PROJ, PROJ))
                moments_of(b, u_b, 2)
                normalise(b, n2_sb, u_b, 2, n2_done)
            blocks(dve, body)

        @block.tensor
        def _(pe):
            pe.wait_ge(s_w, 16 * 4)
            pe.wait_ge(s_const, 9)

            def common_free(b, kind, k):
                alone = isinstance(b, int) and b == -1
                if k >= 2:
                    prev = common_use(b, kind, k - 2)
                elif kind == "norm" or (kind == "proj" and is_last(b)):
                    if alone:
                        return
                    wait(pe, act_took, took_at(b, k - 1))
                    return
                elif kind == "proj":
                    prev = common_use(b, "norm", NORM_T - 2 + k)
                elif kind == "qkv":
                    prev = common_use(b, "norm" if alone else "proj", NORM_T - 2 + k)
                else:
                    prev = common_use(b, "proj", PROJ - 2 + k) if is_last(b) else common_use(b, "qkv", QKV - 2 + k)
                wait(pe, prev[1], prev[2])

            def turn_norm(b, kind, src, k4s):
                for k4 in k4s:
                    common_free(b, kind, k4)
                    k, t4 = k4 // 4, k4 % 4
                    for s in range(4):
                        ins = nc.tensor.transpose(common[:, k4 % 2, s * P:(s + 1) * P],
                                                  src[:, 4 * t4 + s, k * P:(k + 1) * P], ident[:])
                    ins.then_inc(made, 1)

            def make_qkv(b):
                wait(pe, act_took, common_use(b, "norm", NORM_T - 1)[2])
                for use in range(QKV):
                    common_free(b, "qkv", use)
                    m, t4 = use // 4, use % 4
                    for k in range(KH):
                        ins = nc.tensor.matmul(common[:, use % 2], w_qkv[:, k, m * P:(m + 1) * P],
                                               xT[:, k, 4 * t4:4 * t4 + 4].rearrange("p s l -> p (s l)"),
                                               start=(k == 0), stop=(k == KH - 1))
                    ins.then_inc(made, 1)

            wait(pe, n1_done, 1)
            turn_norm(-1, "norm", n1, range(NORM_T))
            make_qkv(-1)

            def body(b):
                def scores(i):
                    wait(pe, act_took, qkv_taken(b))
                    wait(pe, kx_done, at(b, GROUPS, i + 1))
                    wait(pe, soft, at(b, 6 * GROUPS, 6 * (i - 2) + 1))
                    for l in range(GL):
                        r, col = 32 * (l % 4), P * (l // 4)
                        ins = nc.tensor.matmul(score[r:r + 32, i % 2, col:col + P],
                                               qT[:, :, :, i * GL + l].rearrange("p a s -> p (a s)"),
                                               kx[:, i % 2, l].rearrange("p g t -> p (g t)"), start=True, stop=True)
                    ins.then_inc(score_made, 1)

                def turn_values(i):
                    if i in POOL_SPREADS:
                        wait(pe, vx_by_pool, at(b, len(POOL_SPREADS), POOL_SPREADS.index(i) + 1))
                    else:
                        wait(pe, vx_by_vector, at(b, len(VECTOR_SPREADS), VECTOR_SPREADS.index(i) + 1))
                    for k in range(4):
                        wait(pe, vbd_done, at(b, 4 * GROUPS, 4 * i + k - 1))
                        for l in range(4):
                            ins = nc.tensor.transpose(vbank[:, k % 2, l * P:(l + 1) * P],
                                                      vx[:, i % 2, 4 * k + l].rearrange("p g t -> p (g t)"), ident[:])
                        ins.then_inc(vbank_made, 1)

                def turn_probs(i):
                    wait(pe, soft, at(b, 6 * GROUPS, 6 * i + 6))
                    wait(pe, pbank_took, at(b, GROUPS + 1, i))
                    wait(pe, o_done, at(b, GROUPS, i - 1))
                    for k in range(4):
                        ins = nc.tensor.transpose(pbank[:, k * P:(k + 1) * P],
                                                  sm[:, i % 2, k * KV:(k + 1) * KV].rearrange("p g t -> p (g t)"), ident[:])
                    ins.then_inc(pbank_made, 1)

                def outputs(i):
                    wait(pe, pbank_took, at(b, GROUPS + 1, i + 1))
                    wait(pe, vbd_done, at(b, 4 * GROUPS, 4 * i + 4))
                    wait(pe, rows_done, at(b, GROUPS, i))
                    for l in range(GL):
                        r, col = 32 * (l % 4), P * (l // 4)
                        ins = nc.tensor.matmul(obank[r:r + 32, col:col + P], pT[:, i % 2, 32 * l:32 * l + 32],
                                               vbd[:, i % 2, l], start=True, stop=True)
                    ins.then_inc(obank_made, 1)

                def turn_output(i):
                    wait(pe, rows_done, at(b, GROUPS, i + 1))
                    if i < GROUPS - 1:
                        wait(pe, pbank_took, at(b, GROUPS + 1, i + 2))
                    else:
                        wait(pe, o_done, at(b, GROUPS, i))
                    for k in range(4):
                        ins = nc.tensor.transpose(pbank[:, k * P:(k + 1) * P], o_rows[:, i % 2, k * P:(k + 1) * P], ident[:])
                    ins.then_inc(turned, 1)

                for i in range(GROUPS):
                    scores(i)
                    if i:
                        turn_probs(i - 1)
                    turn_values(i)
                    if i:
                        outputs(i - 1)
                    if i >= 2:
                        turn_output(i - 2)
                turn_probs(GROUPS - 1)
                outputs(GROUPS - 1)
                turn_output(GROUPS - 2)
                turn_output(GROUPS - 1)
                if not is_last(b):
                    wait(pe, n1_done, at(b, 1, 2))
                    turn_norm(b, "norm", n1, range(NORM_T))
                wait(pe, o_done, at(b, GROUPS, GROUPS))
                for i in range(PROJ):
                    common_free(b, "proj", i)
                    for j in range(2):
                        for a in range(PAIR):
                            ins = nc.tensor.matmul(common[:, i % 2, j * H:(j + 1) * H], oT[:, a, 2 * i + j],
                                                   w_proj[:, a], start=(a == 0), stop=(a == PAIR - 1))
                    ins.then_inc(made, 1)
                if not is_last(b):
                    make_qkv(b)
                wait(pe, n2_done, at(b, 1, 1))
                turn_norm(b, "norm2", n2_sb, range(NORM2_T))
                last_norm = common_use(b, "norm2", NORM2_T - 1)
                wait(pe, last_norm[1], last_norm[2])
                wait(pe, pbank_took, at(b, GROUPS + 1, GROUPS))
                for s in range(S):
                    for k in range(KH):
                        ins = nc.tensor.matmul(pbank[:, s * EXPERTS:(s + 1) * EXPERTS], xT[:, k, s], w_router[:, k],
                                               start=(k == 0), stop=(k == KH - 1))
                ins.then_inc(pbank_made, 1)
            blocks(pe, body)


def routing_stage(nc, logits, slot_of, weight_of):
    TILES = TOKENS // P
    B = L // P
    E = EXPERTS
    with ExitStack() as ctx:
        al = Allocator(nc, ctx, "r_")
        sb, sem = al.sb, al.sem
        raw = sb("raw", [P, B, S, E])
        prob = sb("prob", [P, TILES, E])
        best = [sb("best0", [P, TILES, E]), sb("best1", [P, TILES, E])]
        work = sb("work", [P, TILES, E])
        rank = sb("rank", [P, TILES, E])
        chosen = sb("chosen", [P, TILES, E])
        top = sb("top", [P, TOPK, TILES])
        line = sb("line", [P, TILES])
        kept = sb("kept", [P, TOPK, TILES])
        slot_f = sb("slot_f", [P, TOPK, TILES])
        desc = sb("desc", [P, E])
        first_slot = sb("first_slot", [P, E])
        ones = sb("ones", [P, P])
        earlier = sb("earlier", [P, P])
        within = al.ps("within", [P, TILES, E])
        total = al.ps("total", [P, TILES, E])
        loaded = sem("loaded")
        const = sem("const")
        step = sem("step")
        exped = sem("exped")
        counted = sem("counted")
        CONST = 3 + 2 * E
        STEP_CHOSEN = 19
        block = ctx.enter_context(nc.Block())

        @block.sync
        def _(sp):
            sp.dma_start(raw[:], logits.rearrange("b p s e -> p b s e")).then_inc(loaded, 16)

        @block.gpsimd
        def _(pool):
            nc.gpsimd.memset(ones[:], 1.0).then_inc(const, 1)
            nc.gpsimd.memset(earlier[:], 1.0).then_inc(const, 1)
            for e in range(E):
                nc.gpsimd.memset(desc[:, e:e + 1], float(E - e)).then_inc(const, 1)
                nc.gpsimd.memset(first_slot[:, e:e + 1], float(e * CAP)).then_inc(const, 1)
            pool.wait_ge(const, 2)
            nc.gpsimd.affine_select(out=earlier[:], in_=earlier[:], compare_op=ALU.is_gt, fill=0.0,
                                    base=0, pattern=[[1, P]], channel_multiplier=-1).then_inc(const, 1)
        @block.scalar
        def _(act):
            act.wait_ge(step, 3)
            nc.scalar.activation(prob[:], prob[:], ACT.Exp).then_inc(exped, 1)

        @block.tensor
        def _(pe):
            pe.wait_ge(const, CONST)
            pe.wait_ge(step, STEP_CHOSEN)
            for half in range(2):
                part = slice(half * TILES // 2, (half + 1) * TILES // 2)
                nc.tensor.matmul(within[:, part].rearrange("p t e -> p (t e)"), earlier[:],
                                 chosen[:, part].rearrange("p t e -> p (t e)"), start=True, stop=True)
                ins = nc.tensor.matmul(total[:, part].rearrange("p t e -> p (t e)"), ones[:],
                                       chosen[:, part].rearrange("p t e -> p (t e)"), start=True, stop=True)
            ins.then_inc(counted, 1)

        @block.vector
        def _(dve):
            n = [0]

            def after_last(ins):
                n[0] += 1
                ins.then_inc(step, 1)
                dve.wait_ge(step, n[0])

            def per_token(x):
                return x.unsqueeze(2).to_broadcast([P, TILES, E])

            def per_expert(x):
                return x.unsqueeze(1).to_broadcast([P, TILES, E])

            tt = nc.vector.tensor_tensor
            dve.wait_ge(const, CONST)
            dve.wait_ge(loaded, 16)
            after_last(nc.vector.tensor_copy(prob[:].rearrange("p (s b) e -> p b s e", b=B), raw[:]))
            after_last(nc.vector.reduce_max(line[:], prob[:], axis=AXX))
            after_last(tt(prob[:], prob[:], per_token(line[:]), ALU.subtract))
            dve.wait_ge(exped, 1)
            after_last(nc.vector.reduce_sum(line[:], prob[:], axis=AXX))
            after_last(nc.vector.reciprocal(line[:], line[:]))
            after_last(tt(prob[:], prob[:], per_token(line[:]), ALU.mult))
            for k in range(TOPK):
                after_last(nc.vector.reduce_max(top[:, k], prob[:], axis=AXX))
                after_last(tt(work[:], prob[:], per_token(top[:, k]), ALU.is_equal))
                after_last(tt(work[:], work[:], per_expert(desc[:]), ALU.mult))
                after_last(nc.vector.reduce_max(line[:], work[:], axis=AXX))
                after_last(tt(best[k][:], per_token(line[:]), per_expert(desc[:]), ALU.is_equal))
                if k == 0:
                    after_last(nc.vector.scalar_tensor_tensor(out=prob[:], in0=best[0][:], scalar=-2.0, in1=prob[:],
                                                              op0=ALU.mult, op1=ALU.add))
            after_last(tt(chosen[:], best[0][:], best[1][:], ALU.add))
            after_last(tt(line[:], top[:, 0], top[:, 1], ALU.add))
            assert n[0] == STEP_CHOSEN, n
            after_last(nc.vector.reciprocal(line[:], line[:]))
            for k in range(TOPK):
                after_last(tt(top[:, k], top[:, k], line[:], ALU.mult))
            dve.wait_ge(counted, 1)
            for e in range(E):
                ins = nc.vector.tensor_tensor_scan(rank[:, :, e], ones[:, 0:TILES], total[:, :, e], 0.0,
                                                   ALU.mult, ALU.add)
            after_last(ins)
            after_last(tt(rank[:], rank[:], total[:], ALU.subtract))
            after_last(tt(rank[:], rank[:], within[:], ALU.add))
            after_last(nc.vector.tensor_scalar(work[:], rank[:], float(CAP), None, ALU.is_lt))
            after_last(tt(rank[:], rank[:], per_expert(first_slot[:]), ALU.add))
            for k in range(TOPK):
                after_last(tt(prob[:], best[k][:], work[:], ALU.mult))
                after_last(nc.vector.reduce_sum(kept[:, k], prob[:], axis=AXX))
                after_last(tt(prob[:], best[k][:], rank[:], ALU.mult))
                after_last(nc.vector.reduce_sum(slot_f[:, k], prob[:], axis=AXX))
            after_last(tt(weight_of[:], top[:], kept[:], ALU.mult))
            after_last(nc.vector.scalar_tensor_tensor(out=slot_f[:], in0=slot_f[:], scalar=float(-SLOTS), in1=kept[:],
                                                      op0=ALU.add, op1=ALU.mult))
            after_last(nc.vector.tensor_scalar(slot_f[:], slot_f[:], float(SLOTS), None, ALU.add))
            after_last(nc.vector.tensor_copy(slot_of[:], slot_f[:]))


def in_pairs(eng, body):
    body(0)
    with eng.Fori(1, S // 2 - 1) as pair:
        body(pair)
    body(S // 2 - 1)


def dispatch_stage(nc, n2, slot_of, slot_rows):
    B = L // P
    with ExitStack() as ctx:
        al = Allocator(nc, ctx, "d_")
        rows = al.sb("rows", [P, 2, B, H])
        index = al.sb("index", [P, 2, TOPK, B], I32)
        loaded = [al.sem("loaded0"), al.sem("loaded1")]
        scattered = [al.sem("scattered0"), al.sem("scattered1")]
        indexed = al.sem("indexed")
        passed, passed_pool = al.sem("passed"), al.sem("passed_pool")
        PER_S = 16 * TOPK * B
        block = ctx.enter_context(nc.Block())

        @block.sync
        def _(sp):
            def body(pair):
                for half in range(2):
                    wait_apart(sp, scattered[half], pair * PER_S, passed)
                    sp.dma_start(rows[:, half], n2.rearrange("s (b p) m -> s p b m", p=P)[2 * pair + half]).then_inc(loaded[half], 16)
            in_pairs(sp, body)

        @block.vector
        def _(dve):
            def body(pair):
                for half in range(2):
                    wait(dve, scattered[half], pair * PER_S)
                    col = pair * (2 * B) + half * B
                    nc.vector.tensor_copy(index[:, half], slot_of[:, :, bass.ds(col, B)]).then_inc(indexed, 1)
            in_pairs(dve, body)

        @block.gpsimd
        def _(pool):
            def body(pair):
                for half in range(2):
                    wait(pool, loaded[half], pair * 16 + 16)
                    wait_apart(pool, indexed, pair * 2 + (half + 1), passed_pool)
                    for b in range(B):
                        for k in range(TOPK):
                            nc.gpsimd.indirect_dma_start(
                                slot_rows, bass.IndirectOffsetOnAxis(ap=index[:, half, k, b:b + 1], axis=0),
                                rows[:, half, b], None, bounds_check=SLOTS - 1, oob_is_err=False).then_inc(scattered[half], 16)
            in_pairs(pool, body)
            for half in range(2):
                pool.wait_ge(scattered[half], S // 2 * PER_S)


def expert_stage(nc, w, slot_rows, slot_out):
    SB = 512
    BLOCKS = CAP // SB
    FC = FFN // P
    Y_START, T_START = 2 + 2 * BLOCKS, 4
    with ExitStack() as ctx:
        al = Allocator(nc, ctx, "e_")
        sb, sem = al.sb, al.sem
        w1 = sb("w1", [P, 2, KH, FFN])
        w2 = sb("w2", [P, 2, FC, H])
        ln2 = sb("ln2", [P, 4, KH])
        ident = sb("ident", [P, P])
        xe = sb("xe", [P, 2, 4, H])
        xT = sb("xT", [P, 2, KH, SB])
        a = sb("a", [P, 2, FC, SB])
        ye = sb("ye", [P, 2, 4, H])
        tbank = al.ps("tbank", [P, 2, SB])
        ubank = al.ps("ubank", [P, 2, SB])
        ybank = al.ps("ybank", [P, 2, 4, H])
        ln_loaded = sem("ln_loaded")
        w_loaded = [sem("w_loaded0"), sem("w_loaded1")]
        x_loaded = [sem("x_loaded0"), sem("x_loaded1")]
        const = sem("const")
        t_made, t_free = sem("t_made"), sem("t_free")
        u_made, u_taken = sem("u_made"), sem("u_taken")
        y_made, y_free = sem("y_made"), sem("y_free")
        y_stored, ye_free = sem("y_stored"), sem("ye_free")
        sp_passed = sem("sp_passed")
        pool_passed, pe_passed = sem("pool_passed"), sem("pe_passed")
        x_b = slot_rows.rearrange("(n j p) m -> n p j m", j=4, p=P)
        y_b = slot_out[0:SLOTS, :].rearrange("(n j p) m -> n p j m", j=4, p=P)
        w1_e = w["w1"].rearrange("e (k p) f -> e p k f", p=P)
        w2_e = w["w2"].rearrange("e (c p) m -> e p c m", p=P)
        block = ctx.enter_context(nc.Block())

        def each_block(eng, body, expert=None):
            with eng.Fori(0, EXPERTS // 2) as pair:
                for half in range(2):
                    if expert:
                        expert(pair, half)
                    with eng.Fori(0, BLOCKS // 2) as two:
                        for sub in range(2):
                            body(pair * BLOCKS + two + half * (BLOCKS // 2), half, sub)

        @block.sync
        def _(sp):
            sp.dma_start(ln2[:], w["ln_vecs"]).then_inc(ln_loaded, 16)
            sp.dma_start(xe[:, 0], x_b[0]).then_inc(x_loaded[0], 16)

            def weights(pair, half):
                e = pair * 2 + half
                wait_apart(sp, y_free, e * BLOCKS + (Y_START - BLOCKS), sp_passed)
                sp.dma_start(w1[:, half], w1_e[e]).then_inc(w_loaded[half], 16)
                sp.dma_start(w2[:, half], w2_e[e]).then_inc(w_loaded[half], 16)

            def body(m, half, sub):
                n = m * 2 + sub
                wait_apart(sp, t_free, n * 2 + T_START, sp_passed)
                sp.dma_start(xe[:, 1 - sub], x_b[n + 1]).then_inc(x_loaded[1 - sub], 16)
            each_block(sp, body, weights)

        @block.gpsimd
        def _(pool):
            nc.gpsimd.memset(ident[:], 0.0).then_inc(const, 1)
            pool.wait_ge(const, 1)
            nc.gpsimd.affine_select(out=ident[:], in_=ident[:], compare_op=ALU.not_equal, fill=1.0,
                                    base=0, pattern=[[-1, P]], channel_multiplier=1).then_inc(const, 1)
            pool.sem_inc(ye_free, 2)

            def body(m, half, sub):
                n = m * 2 + sub
                wait_apart(pool, y_free, n + (Y_START + 1), pool_passed)
                nc.gpsimd.dma_start(y_b[n], ye[:, sub]).then_inc(y_stored, 16)
                wait(pool, y_stored, n * 16 + 16)
                pool.sem_inc(ye_free, 1)
            each_block(pool, body)

        @block.scalar
        def _(act):
            act.wait_ge(ln_loaded, 16)
            act.sem_inc(t_free, T_START)
            act.sem_inc(u_taken, 2)

            def take_rows(n, sub):
                for k in range(KH):
                    wait(act, t_made, n * 2 + (k + 1))
                    nc.scalar.activation(xT[:, sub, k], tbank[:, k], ACT.Identity, scale=ln2[:, 2, k:k + 1],
                                         bias=ln2[:, 3, k:k + 1]).then_inc(t_free, 1)

            take_rows(0, 0)

            def body(m, half, sub):
                n = m * 2 + sub
                for c in range(FC):
                    wait(act, u_made, n * FC + (c + 1))
                    nc.scalar.activation(a[:, sub, c], ubank[:, c % 2], ACT.Gelu).then_inc(u_taken, 1)
                take_rows(n + 1, 1 - sub)
            each_block(act, body)

        @block.vector
        def _(dve):
            dve.sem_inc(y_free, Y_START)

            def body(m, half, sub):
                n = m * 2 + sub
                wait(dve, y_made, n + 1)
                wait(dve, ye_free, n + 1)
                nc.vector.tensor_copy(ye[:, sub], ybank[:, sub]).then_inc(y_free, 1)
            each_block(dve, body)

        @block.tensor
        def _(pe):
            pe.wait_ge(const, 2)

            def turn_rows(n, turn, sub):
                wait(pe, x_loaded[sub], turn * 16 + 16)
                for k in range(KH):
                    wait(pe, t_free, n * 2 + (k + T_START - 1))
                    for j in range(4):
                        ins = nc.tensor.transpose(tbank[:, k, j * P:(j + 1) * P], xe[:, sub, j, k * P:(k + 1) * P], ident[:])
                    ins.then_inc(t_made, 1)

            turn_rows(0, 0, 0)

            def weights(pair, half):
                wait_apart(pe, w_loaded[half], pair * 32 + 32, pe_passed)

            def body(m, half, sub):
                n = m * 2 + sub
                wait(pe, t_free, n * 2 + (T_START + 2))
                for c in range(FC):
                    wait(pe, u_taken, n * FC + (c + 1))
                    for k in range(KH):
                        ins = nc.tensor.matmul(ubank[:, c % 2], w1[:, half, k, c * P:(c + 1) * P], xT[:, sub, k],
                                               start=(k == 0), stop=(k == KH - 1))
                    ins.then_inc(u_made, 1)
                turn_rows(n + 1, m + sub, 1 - sub)
                wait(pe, u_taken, n * FC + (FC + 2))
                wait(pe, y_free, n + (Y_START - 1))
                for j in range(4):
                    for c in range(FC):
                        ins = nc.tensor.matmul(ybank[:, sub, j], a[:, sub, c, j * P:(j + 1) * P], w2[:, half, c],
                                               start=(c == 0), stop=(c == FC - 1))
                ins.then_inc(y_made, 1)
            each_block(pe, body, weights)


def combine_stage(nc, base, slot_out, slot_of, weight_of, out):
    B = L // P
    with ExitStack() as ctx:
        al = Allocator(nc, ctx, "c_")
        rows = al.sb("rows", [P, 2, B, H])
        got = al.sb("got", [P, 2, TOPK, B, H])
        index = al.sb("index", [P, 2, TOPK, B], I32)
        weight = al.sb("weight", [P, 2, TOPK, B])
        loaded = [al.sem("loaded0"), al.sem("loaded1")]
        gathered = [al.sem("gathered0"), al.sem("gathered1")]
        stored = [al.sem("stored0"), al.sem("stored1")]
        indexed, first_added, summed = al.sem("indexed"), al.sem("first_added"), al.sem("summed")
        sp_passed, pool_passed, act_passed = al.sem("sp_passed"), al.sem("pool_passed"), al.sem("act_passed")
        PER_S = 16 * TOPK * B
        base_s = base.rearrange("s (b p) m -> s p b m", p=P)
        out_s = out.rearrange("s (b p) m -> s p b m", p=P)
        block = ctx.enter_context(nc.Block())

        @block.sync
        def _(sp):
            def body(pair):
                for half in range(2):
                    wait_apart(sp, stored[half], pair * 16, sp_passed)
                    sp.dma_start(rows[:, half], base_s[2 * pair + half]).then_inc(loaded[half], 16)
            in_pairs(sp, body)

        @block.scalar
        def _(act):
            def body(pair):
                for half in range(2):
                    wait_apart(act, summed, pair * 2 + (half + 1), act_passed)
                    nc.scalar.dma_start(out_s[2 * pair + half], rows[:, half]).then_inc(stored[half], 16)
            in_pairs(act, body)
            for half in range(2):
                act.wait_ge(stored[half], 16 * S // 2)

        @block.gpsimd
        def _(pool):
            def body(pair):
                for half in range(2):
                    wait(pool, summed, pair * 2 + (half - 1))
                    wait_apart(pool, indexed, pair * 4 + 2 * (half + 1), pool_passed)
                    for b in range(B):
                        for k in range(TOPK):
                            nc.gpsimd.indirect_dma_start(
                                got[:, half, k, b], None, slot_out,
                                bass.IndirectOffsetOnAxis(ap=index[:, half, k, b:b + 1], axis=0)).then_inc(gathered[half], 16)
            in_pairs(pool, body)

        @block.vector
        def _(dve):
            def take_index(pair, half):
                wait(dve, gathered[half], pair * PER_S)
                wait(dve, summed, pair * 2 + (half - 1))
                col = pair * (2 * B) + half * B
                nc.vector.tensor_copy(index[:, half], slot_of[:, :, bass.ds(col, B)]).then_inc(indexed, 1)
                nc.vector.tensor_copy(weight[:, half], weight_of[:, :, bass.ds(col, B)]).then_inc(indexed, 1)

            def body(pair, ahead):
                for half in range(2):
                    wait(dve, loaded[half], pair * 16 + 16)
                    wait(dve, gathered[half], pair * PER_S + PER_S)
                    wait(dve, indexed, pair * 4 + 2 * (half + 1))
                    for k in range(TOPK):
                        if k:
                            wait(dve, first_added, pair * 2 + (half + 1))
                        for b in range(B):
                            ins = nc.vector.scalar_tensor_tensor(
                                out=rows[:, half, b], in0=got[:, half, k, b], scalar=weight[:, half, k, b:b + 1],
                                in1=rows[:, half, b], op0=ALU.mult, op1=ALU.add)
                        ins.then_inc(summed if k else first_added, 1)
                    if ahead:
                        take_index(pair + 1, half)

            for half in range(2):
                take_index(0, half)
            with dve.Fori(0, S // 2 - 1) as pair:
                body(pair, True)
            body(S // 2 - 1, False)


def build(nc, t, out):
    def scratch(name, shape):
        return nc.dram_tensor(name, shape, F32, kind="Internal").ap()

    x1 = scratch("x1", (S, L, H))
    base = scratch("base", (S, L, H))
    n2 = scratch("n2", (S, L, H))
    logits = scratch("logits", (L // P, P, S, EXPERTS))
    slot_rows = scratch("slot_rows", (SLOTS + 512, H))
    slot_out = scratch("slot_out", (SLOTS + P, H))
    mamba_stage(nc, t["x"], t, x1)
    attention_stage(nc, x1, t, base, n2, logits, slot_rows, slot_out)
    with nc.sbuf_tensor("slot_of", [P, TOPK, TOKENS // P], I32) as slot_of, \
            nc.sbuf_tensor("weight_of", [P, TOPK, TOKENS // P], F32) as weight_of:
        routing_stage(nc, logits, slot_of, weight_of)
        dispatch_stage(nc, n2, slot_of, slot_rows)
        expert_stage(nc, t, slot_rows, slot_out)
        combine_stage(nc, base, slot_out, slot_of, weight_of, out)


def kernel(**inputs):
    import numpy as _np
    import concourse.bacc as _bacc
    from concourse.bass_utils import run_bass_kernel_spmd as _run

    g = {k: _np.asarray(v) for k, v in inputs.items()}
    m, f = "L0_attn_", "L0_ffn_"
    qkv = g[f + "qkv_weight"].reshape(KV, HEADS // KV + 2, HD, H)
    proj = g[f + "proj_weight"].T.reshape(KV, HEADS // KV, HD, H)
    arrays = {
        "x": g[m + "hidden_states"],
        "in_T": g[m + "in_proj_w"].T,
        "x_T": g[m + "x_proj_w"].T,
        "dt_T": g[m + "dt_proj_w"].T,
        "out_T": g[m + "out_proj_w"].T,
        "A_log": g[m + "A_log"],
        "conv_w": g[m + "conv_w"],
        "vecs": _np.stack([g[m + n].reshape(CH, P).T for n in ("conv_b", "dt_proj_b", "D")]),
        "qkv_T": qkv.transpose(1, 0, 2, 3).reshape(4 * P, H).T,
        "proj_T": proj.transpose(1, 0, 2, 3).reshape(2 * P, H),
        "router": g[f + "router_weight"],
        "ln_vecs": _np.stack([g[f + n] for n in ("ln1_weight", "ln1_bias", "ln2_weight", "ln2_bias")]
                             ).reshape(4, KH, P).transpose(2, 0, 1),
        "w1": g[f + "moe_w1"],
        "w2": g[f + "moe_w2"],
    }
    arrays = {k: _np.ascontiguousarray(a) for k, a in arrays.items()}
    nc = _bacc.Bacc("TRN2", target_bir_lowering=False, num_devices=1)
    t = {k: nc.dram_tensor("in_" + k, a.shape, F32, kind="ExternalInput").ap() for k, a in arrays.items()}
    out = nc.dram_tensor("out", (S, L, H), F32, kind="ExternalOutput").ap()
    build(nc, t, out)
    r = _run(nc, [{"in_" + k: a for k, a in arrays.items()}], core_ids=[0])
    return r.results[0]["out"]
```
